# Optimizing a Trainium2 kernel written in Bass

```python
import numpy as np
import jax
import jax.numpy as jnp

def _softmax(x, axis=-1):
    return jax.nn.softmax(x, axis=axis)

def _gelu(x):
    return jax.nn.gelu(x, approximate=True)

def _silu(x):
    return jax.nn.silu(x)

def _sigmoid(x):
    return jax.nn.sigmoid(x)

def _layernorm(x, axis=-1, eps=1e-05):
    m = jnp.mean(x, axis=axis, keepdims=True)
    v = jnp.var(x, axis=axis, keepdims=True)
    return (x - m) / jnp.sqrt(v + eps)

def _scatter_add(tgt, idx, src, axis=0):
    return tgt.at[idx].add(src)

def _segment_sum(src, seg, n):
    return jax.ops.segment_sum(src, seg, n)
kernel_name = 'mk_decoder_postln_d2_seqx_r8_207134'

def setup_inputs(seed: int=0):
    np.random.seed(seed)
    _w = jnp.asarray

    def _rec_inputs():
        import jax
        import jax.numpy as jnp
        _rk = jax.random.key(seed)
        x = -0.0002928 + 1 * jax.random.normal(jax.random.fold_in(_rk, 1), (64, 128, 128), jnp.float32)
        _lenS = 128 - jax.random.randint(jax.random.fold_in(_rk, 7), (64,), 0, max(1, 128 // 4) + 1, jnp.int32)
        _lenS2 = 77 - jax.random.randint(jax.random.fold_in(_rk, 8), (64,), 0, max(1, 77 // 4) + 1, jnp.int32)
        _ctx_512P = jax.random.normal(jax.random.fold_in(_rk, 11), (64, 16, 64), jnp.float32)
        _ctx_512c = jax.random.dirichlet(jax.random.fold_in(_rk, 511), 0.3 * jnp.ones((16,), jnp.float32), (64, 77))
        _ctx_512t = jnp.einsum('bsk,bkd->bsd', _ctx_512c, _ctx_512P)
        _ctx_512t = _ctx_512t * jax.lax.rsqrt(jnp.mean(jnp.square(_ctx_512t)) + 1e-12) * 0.953939
        ctx_512 = 0.00222621 + 0.99962 * (_ctx_512t + 0.3 * jax.random.normal(jax.random.fold_in(_rk, 611), (64, 77, 64), jnp.float32))
        return (x, ctx_512)
    x, ctx_512 = _rec_inputs()

    def _L0_attn_setup():
        import jax, jax.numpy as jnp
        import numpy as np
        D_MODEL = 128
        D_STATE = 16
        EXPAND = 2
        D_INNER = D_MODEL * EXPAND
        DT_RANK = D_MODEL // 16

        def _ssm_forward(u, W_in, b_in, W_x, b_x, W_dt, b_dt, A_log, D, W_out, b_out):
            B, T, _ = u.shape
            u_inner = u @ W_in.T + b_in
            x, z = jnp.split(u_inner, 2, axis=-1)
            dbc = x @ W_x.T + b_x
            delta_raw = dbc[..., :DT_RANK]
            B_ssm = dbc[..., DT_RANK:DT_RANK + D_STATE]
            C_ssm = dbc[..., DT_RANK + D_STATE:]
            delta = jax.nn.softplus(delta_raw @ W_dt.T + b_dt)
            A = -jnp.exp(A_log)

            def step(h, xs):
                dt_t, x_t, Bt, Ct = xs
                dA = jnp.exp(dt_t[..., None] * A)
                dB = dt_t[..., None] * Bt[:, None, :]
                h = h * dA + x_t[..., None] * dB
                y_t = jnp.einsum('bdn,bn->bd', h, Ct)
                return (h, y_t)
            h0 = jnp.zeros((B, D_INNER, D_STATE), u.dtype)
            xs = (jnp.swapaxes(delta, 0, 1), jnp.swapaxes(x, 0, 1), jnp.swapaxes(B_ssm, 0, 1), jnp.swapaxes(C_ssm, 0, 1))
            _, y = jax.lax.scan(step, h0, xs)
            y = jnp.swapaxes(y, 0, 1)
            y = y + x * D
            y = y * (z * jax.nn.sigmoid(z))
            return y @ W_out.T + b_out
        key = jax.random.key(seed)
        ks = jax.random.split(key, 12)
        B, T = (2, 256)
        s_in = 1.0 / np.sqrt(D_MODEL)
        s_x = 1.0 / np.sqrt(D_INNER)
        s_dt = 1.0 / np.sqrt(DT_RANK)
        inp = {'u': jax.random.normal(ks[0], (B, T, D_MODEL), jnp.float32), 'W_in': jax.random.uniform(ks[1], (2 * D_INNER, D_MODEL), jnp.float32, -s_in, s_in), 'b_in': jax.random.uniform(ks[2], (2 * D_INNER,), jnp.float32, -s_in, s_in), 'W_x': jax.random.uniform(ks[3], (DT_RANK + 2 * D_STATE, D_INNER), jnp.float32, -s_x, s_x), 'b_x': jax.random.uniform(ks[4], (DT_RANK + 2 * D_STATE,), jnp.float32, -s_x, s_x), 'W_dt': jax.random.uniform(ks[5], (D_INNER, DT_RANK), jnp.float32, -s_dt, s_dt), 'b_dt': jax.random.uniform(ks[6], (D_INNER,), jnp.float32, -s_dt, s_dt), 'A_log': jnp.log(jnp.abs(jax.random.normal(ks[7], (D_INNER, D_STATE), jnp.float32)) + 1e-06), 'D': jnp.ones((D_INNER,), jnp.float32), 'W_out': jax.random.uniform(ks[8], (D_MODEL, D_INNER), jnp.float32, -s_x, s_x), 'b_out': jax.random.uniform(ks[9], (D_MODEL,), jnp.float32, -s_x, s_x)}
        return inp
    _L0_attn_all = _L0_attn_setup()
    _L0_attn_in = {k: v for k, v in _L0_attn_all.items() if k in ('W_in', 'b_in', 'W_x', 'b_x', 'W_dt', 'b_dt', 'A_log', 'D', 'W_out', 'b_out')}
    del _L0_attn_all

    def _L0_xattn_setup():
        import jax, jax.numpy as jnp
        import numpy as np
        H, D, C1, C2, S, M, B, W = (16, 32, 128, 64, 256, 64, 2, 4)

        def _ln(x, g, b):
            m = jnp.mean(x, -1, keepdims=True)
            v = jnp.var(x, -1, keepdims=True)
            return (x - m) * jax.lax.rsqrt(v + 1e-05) * g + b

        def _mha(x, y, wq, wk, wv, li1_w, li1_b, lnx_g, lnx_b, lny_g, lny_b, ln3_g, ln3_b, li2_w, li2_b, li3_w, li3_b, causal):
            xn = _ln(x, lnx_g, lnx_b)
            yn = _ln(y, lny_g, lny_b)
            q = jnp.einsum('bsc,hcd->bhsd', xn, wq)
            k = jnp.einsum('btc,hcd->bhtd', yn, wk)
            v = jnp.einsum('btc,hcd->bhtd', yn, wv)
            a = jax.nn.softmax(jnp.einsum('bhsd,bhtd->bhst', q, k) * D ** (-0.5), axis=-1)
            if causal:
                s, t = (a.shape[-2], a.shape[-1])
                mask = (jnp.arange(t)[None, :] > jnp.arange(s)[:, None]).astype(a.dtype)
                a = a * mask
            o = jnp.einsum('bhst,bhtd->bhsd', a, v)
            o = o.transpose(0, 2, 1, 3).reshape(x.shape[0], x.shape[1], H * D)
            x_out = x + o @ li1_w + li1_b
            h = jax.nn.gelu(_ln(x_out, ln3_g, ln3_b) @ li2_w + li2_b, approximate=False)
            return x_out + h @ li3_w + li3_b
        key = jax.random.key(seed)
        ks = iter(jax.random.split(key, 64))

        def w(shape, scale=0.02):
            return jax.random.normal(next(ks), shape, jnp.float32) * scale
        inp = {'xx': jax.random.normal(next(ks), (B, S, C1), jnp.float32), 'ee': jax.random.normal(next(ks), (B, M, C2), jnp.float32), 'ln1_g': jnp.ones(C1, jnp.float32), 'ln1_b': jnp.zeros(C1, jnp.float32), 'ln2_g': jnp.ones(C1, jnp.float32), 'ln2_b': jnp.zeros(C1, jnp.float32)}
        for pfx, cy in (('a1', C1), ('a2', C2)):
            inp[pfx + '_wq'] = w((H, C1, D))
            inp[pfx + '_wk'] = w((H, cy, D))
            inp[pfx + '_wv'] = w((H, cy, D))
            inp[pfx + '_li1_w'] = w((H * D, C1))
            inp[pfx + '_li1_b'] = jnp.zeros(C1, jnp.float32)
            inp[pfx + '_lnx_g'] = jnp.ones(C1, jnp.float32)
            inp[pfx + '_lnx_b'] = jnp.zeros(C1, jnp.float32)
            inp[pfx + '_lny_g'] = jnp.ones(cy, jnp.float32)
            inp[pfx + '_lny_b'] = jnp.zeros(cy, jnp.float32)
            inp[pfx + '_ln3_g'] = jnp.ones(C1, jnp.float32)
            inp[pfx + '_ln3_b'] = jnp.zeros(C1, jnp.float32)
            inp[pfx + '_li2_w'] = w((C1, C1 * W))
            inp[pfx + '_li2_b'] = jnp.zeros(C1 * W, jnp.float32)
            inp[pfx + '_li3_w'] = w((C1 * W, C1))
            inp[pfx + '_li3_b'] = jnp.zeros(C1, jnp.float32)
        inp['training'] = 0
        return inp
    _L0_xattn_all = _L0_xattn_setup()
    _L0_xattn_in = {k: v for k, v in _L0_xattn_all.items() if k in ('ln1_g', 'ln1_b', 'ln2_g', 'ln2_b', 'a1_wq', 'a1_wk', 'a1_wv', 'a1_li1_w', 'a1_li1_b', 'a1_lnx_g', 'a1_lnx_b', 'a1_lny_g', 'a1_lny_b', 'a1_ln3_g', 'a1_ln3_b', 'a1_li2_w', 'a1_li2_b', 'a1_li3_w', 'a1_li3_b', 'a2_wq', 'a2_wk', 'a2_wv', 'a2_li1_w', 'a2_li1_b', 'a2_lnx_g', 'a2_lnx_b', 'a2_lny_g', 'a2_lny_b', 'a2_ln3_g', 'a2_ln3_b', 'a2_li2_w', 'a2_li2_b', 'a2_li3_w', 'a2_li3_b')}
    del _L0_xattn_all

    def _L0_ffn_setup():
        import jax, jax.numpy as jnp
        import numpy as np
        DIM = 128

        def _reference_tuple_inner(x, W_r, W_k, W_v, mu_r, mu_k):
            B, T, C = x.shape
            x_prev = jnp.concatenate([jnp.zeros((B, 1, C), x.dtype), x[:, :-1, :]], axis=1)
            xr = mu_r * x + (1.0 - mu_r) * x_prev
            xk = mu_k * x + (1.0 - mu_k) * x_prev
            r = jax.nn.sigmoid(jnp.einsum('btc,dc->btd', xr, W_r))
            k = jnp.einsum('btc,dc->btd', xk, W_k)
            k_act = jnp.square(jax.nn.relu(k))
            out = r * jnp.einsum('btc,dc->btd', k_act, W_v)
            new_state = x[:, -1, :]
            return (out, new_state)
        key = jax.random.key(seed)
        ks = jax.random.split(key, 6)
        B, T, C = (8, 256, DIM)
        x = jax.random.normal(ks[0], (B, T, C), dtype=jnp.float32)
        s = 1.0 / np.sqrt(C)
        W_r = jax.random.uniform(ks[1], (C, C), jnp.float32, -s, s)
        W_k = jax.random.uniform(ks[2], (C, C), jnp.float32, -s, s)
        W_v = jax.random.uniform(ks[3], (C, C), jnp.float32, -s, s)
        mu_r = jax.random.uniform(ks[4], (C,), jnp.float32)
        mu_k = jax.random.uniform(ks[5], (C,), jnp.float32)
        return {'x': x, 'W_r': W_r, 'W_k': W_k, 'W_v': W_v, 'mu_r': mu_r, 'mu_k': mu_k}
    _L0_ffn_all = _L0_ffn_setup()
    _L0_ffn_in = {k: v for k, v in _L0_ffn_all.items() if k in ('W_r', 'W_k', 'W_v', 'mu_r', 'mu_k')}
    del _L0_ffn_all

    def _L1_attn_setup():
        import jax, jax.numpy as jnp
        import numpy as np
        import math
        B, L, D, H = (2, 128, 128, 16)
        d = D // H
        key = jax.random.key(seed)
        ks = jax.random.split(key, 7)
        s = 1.0 / math.sqrt(D)
        sd = 1.0 / math.sqrt(d)
        return {'X': jax.random.normal(ks[0], (B, L, D), jnp.float32), 'q1_w': jax.random.normal(ks[1], (D, D), jnp.float32) * s, 'k1_w': jax.random.normal(ks[2], (D, D), jnp.float32) * s, 'k2_w': jax.random.normal(ks[3], (D, D), jnp.float32) * s, 'gw_w': jax.random.normal(ks[4], (1, d), jnp.float32) * sd, 'sw_w': jax.random.normal(ks[5], (1, d), jnp.float32) * sd, 'c_proj_w': jax.random.normal(ks[6], (D, D), jnp.float32) * s}
    _L1_attn_all = _L1_attn_setup()
    _L1_attn_in = {k: v for k, v in _L1_attn_all.items() if k in ('q1_w', 'k1_w', 'k2_w', 'gw_w', 'sw_w', 'c_proj_w')}
    del _L1_attn_all

    def _L1_xattn_setup():
        import jax, jax.numpy as jnp
        import numpy as np
        HEADS = 16
        D_MODEL = 128
        IMG_MODEL = 64
        D_K = D_MODEL // HEADS
        key = jax.random.key(seed)
        ks = jax.random.split(key, 12)
        B, LQ, LKV = (8, 256, 128)
        s_dm = 1.0 / np.sqrt(D_MODEL)
        s_im = 1.0 / np.sqrt(IMG_MODEL)
        return {'q': jax.random.normal(ks[0], (B, LQ, D_MODEL), jnp.float32), 'k': jax.random.normal(ks[1], (B, LKV, IMG_MODEL), jnp.float32), 'v': jax.random.normal(ks[2], (B, LKV, IMG_MODEL), jnp.float32), 'Wq': jax.random.normal(ks[3], (D_MODEL, D_MODEL), jnp.float32) * s_dm, 'bq': jnp.zeros((D_MODEL,), jnp.float32), 'Wk': jax.random.normal(ks[4], (IMG_MODEL, D_MODEL), jnp.float32) * s_im, 'bk': jnp.zeros((D_MODEL,), jnp.float32), 'Wv': jax.random.normal(ks[5], (IMG_MODEL, D_MODEL), jnp.float32) * s_im, 'bv': jnp.zeros((D_MODEL,), jnp.float32), 'Wo': jax.random.normal(ks[6], (D_MODEL, D_MODEL), jnp.float32) * s_dm, 'bo': jnp.zeros((D_MODEL,), jnp.float32)}
    _L1_xattn_all = _L1_xattn_setup()
    _L1_xattn_in = {k: v for k, v in _L1_xattn_all.items() if k in ('Wq', 'bq', 'Wk', 'bk', 'Wv', 'bv', 'Wo', 'bo')}
    del _L1_xattn_all

    def _L1_ffn_setup():
        import jax, jax.numpy as jnp
        import numpy as np
        B, S, D, F, E = (1, 128, 128, 512, 8)
        EPS = 1e-05

        def _sublayer(xs, g, b, W1e, b1e, W2e, b2e):
            mu = jnp.mean(xs, axis=-1, keepdims=True)
            var = jnp.mean(jnp.square(xs - mu), axis=-1, keepdims=True)
            h = (xs - mu) * jax.lax.rsqrt(var + EPS) * g + b
            return xs + jax.nn.relu(h @ W1e.T + b1e) @ W2e.T + b2e
        key = jax.random.key(seed)
        ks = jax.random.split(key, 4)
        x = jax.random.normal(ks[0], (B, S, D), jnp.float32)
        centroids = jax.random.normal(ks[1], (E, D), jnp.float32) * 0.1
        gamma = jnp.ones((E, D), jnp.float32)
        beta = jnp.zeros((E, D), jnp.float32)
        W1 = jax.random.normal(ks[2], (E, F, D), jnp.float32) * 0.02
        b1 = jnp.zeros((E, F), jnp.float32)
        W2 = jax.random.normal(ks[3], (E, D, F), jnp.float32) * 0.02
        b2 = jnp.zeros((E, D), jnp.float32)
        return {'x': x, 'centroids': centroids, 'gamma': gamma, 'beta': beta, 'W1': W1, 'b1': b1, 'W2': W2, 'b2': b2}
    _L1_ffn_all = _L1_ffn_setup()
    _L1_ffn_in = {k: v for k, v in _L1_ffn_all.items() if k in ('centroids', 'gamma', 'beta', 'W1', 'b1', 'W2', 'b2')}
    del _L1_ffn_all
    return {'x': x, 'ctx_512': ctx_512, 'L0_attn_W_in': _L0_attn_in['W_in'], 'L0_attn_b_in': _L0_attn_in['b_in'], 'L0_attn_W_x': _L0_attn_in['W_x'], 'L0_attn_b_x': _L0_attn_in['b_x'], 'L0_attn_W_dt': _L0_attn_in['W_dt'], 'L0_attn_b_dt': _L0_attn_in['b_dt'], 'L0_attn_A_log': _L0_attn_in['A_log'], 'L0_attn_D': _L0_attn_in['D'], 'L0_attn_W_out': _L0_attn_in['W_out'], 'L0_attn_b_out': _L0_attn_in['b_out'], 'L0_xattn_ln1_g': _L0_xattn_in['ln1_g'], 'L0_xattn_ln1_b': _L0_xattn_in['ln1_b'], 'L0_xattn_ln2_g': _L0_xattn_in['ln2_g'], 'L0_xattn_ln2_b': _L0_xattn_in['ln2_b'], 'L0_xattn_a1_wq': _L0_xattn_in['a1_wq'], 'L0_xattn_a1_wk': _L0_xattn_in['a1_wk'], 'L0_xattn_a1_wv': _L0_xattn_in['a1_wv'], 'L0_xattn_a1_li1_w': _L0_xattn_in['a1_li1_w'], 'L0_xattn_a1_li1_b': _L0_xattn_in['a1_li1_b'], 'L0_xattn_a1_lnx_g': _L0_xattn_in['a1_lnx_g'], 'L0_xattn_a1_lnx_b': _L0_xattn_in['a1_lnx_b'], 'L0_xattn_a1_lny_g': _L0_xattn_in['a1_lny_g'], 'L0_xattn_a1_lny_b': _L0_xattn_in['a1_lny_b'], 'L0_xattn_a1_ln3_g': _L0_xattn_in['a1_ln3_g'], 'L0_xattn_a1_ln3_b': _L0_xattn_in['a1_ln3_b'], 'L0_xattn_a1_li2_w': _L0_xattn_in['a1_li2_w'], 'L0_xattn_a1_li2_b': _L0_xattn_in['a1_li2_b'], 'L0_xattn_a1_li3_w': _L0_xattn_in['a1_li3_w'], 'L0_xattn_a1_li3_b': _L0_xattn_in['a1_li3_b'], 'L0_xattn_a2_wq': _L0_xattn_in['a2_wq'], 'L0_xattn_a2_wk': _L0_xattn_in['a2_wk'], 'L0_xattn_a2_wv': _L0_xattn_in['a2_wv'], 'L0_xattn_a2_li1_w': _L0_xattn_in['a2_li1_w'], 'L0_xattn_a2_li1_b': _L0_xattn_in['a2_li1_b'], 'L0_xattn_a2_lnx_g': _L0_xattn_in['a2_lnx_g'], 'L0_xattn_a2_lnx_b': _L0_xattn_in['a2_lnx_b'], 'L0_xattn_a2_lny_g': _L0_xattn_in['a2_lny_g'], 'L0_xattn_a2_lny_b': _L0_xattn_in['a2_lny_b'], 'L0_xattn_a2_ln3_g': _L0_xattn_in['a2_ln3_g'], 'L0_xattn_a2_ln3_b': _L0_xattn_in['a2_ln3_b'], 'L0_xattn_a2_li2_w': _L0_xattn_in['a2_li2_w'], 'L0_xattn_a2_li2_b': _L0_xattn_in['a2_li2_b'], 'L0_xattn_a2_li3_w': _L0_xattn_in['a2_li3_w'], 'L0_xattn_a2_li3_b': _L0_xattn_in['a2_li3_b'], 'L0_ffn_W_r': _L0_ffn_in['W_r'], 'L0_ffn_W_k': _L0_ffn_in['W_k'], 'L0_ffn_W_v': _L0_ffn_in['W_v'], 'L0_ffn_mu_r': _L0_ffn_in['mu_r'], 'L0_ffn_mu_k': _L0_ffn_in['mu_k'], 'L1_attn_q1_w': _L1_attn_in['q1_w'], 'L1_attn_k1_w': _L1_attn_in['k1_w'], 'L1_attn_k2_w': _L1_attn_in['k2_w'], 'L1_attn_gw_w': _L1_attn_in['gw_w'], 'L1_attn_sw_w': _L1_attn_in['sw_w'], 'L1_attn_c_proj_w': _L1_attn_in['c_proj_w'], 'L1_xattn_Wq': _L1_xattn_in['Wq'], 'L1_xattn_bq': _L1_xattn_in['bq'], 'L1_xattn_Wk': _L1_xattn_in['Wk'], 'L1_xattn_bk': _L1_xattn_in['bk'], 'L1_xattn_Wv': _L1_xattn_in['Wv'], 'L1_xattn_bv': _L1_xattn_in['bv'], 'L1_xattn_Wo': _L1_xattn_in['Wo'], 'L1_xattn_bo': _L1_xattn_in['bo'], 'L1_ffn_centroids': _L1_ffn_in['centroids'], 'L1_ffn_gamma': _L1_ffn_in['gamma'], 'L1_ffn_beta': _L1_ffn_in['beta'], 'L1_ffn_W1': _L1_ffn_in['W1'], 'L1_ffn_b1': _L1_ffn_in['b1'], 'L1_ffn_W2': _L1_ffn_in['W2'], 'L1_ffn_b2': _L1_ffn_in['b2']}

def reference(x, ctx_512, L0_attn_W_in, L0_attn_b_in, L0_attn_W_x, L0_attn_b_x, L0_attn_W_dt, L0_attn_b_dt, L0_attn_A_log, L0_attn_D, L0_attn_W_out, L0_attn_b_out, L0_xattn_ln1_g, L0_xattn_ln1_b, L0_xattn_ln2_g, L0_xattn_ln2_b, L0_xattn_a1_wq, L0_xattn_a1_wk, L0_xattn_a1_wv, L0_xattn_a1_li1_w, L0_xattn_a1_li1_b, L0_xattn_a1_lnx_g, L0_xattn_a1_lnx_b, L0_xattn_a1_lny_g, L0_xattn_a1_lny_b, L0_xattn_a1_ln3_g, L0_xattn_a1_ln3_b, L0_xattn_a1_li2_w, L0_xattn_a1_li2_b, L0_xattn_a1_li3_w, L0_xattn_a1_li3_b, L0_xattn_a2_wq, L0_xattn_a2_wk, L0_xattn_a2_wv, L0_xattn_a2_li1_w, L0_xattn_a2_li1_b, L0_xattn_a2_lnx_g, L0_xattn_a2_lnx_b, L0_xattn_a2_lny_g, L0_xattn_a2_lny_b, L0_xattn_a2_ln3_g, L0_xattn_a2_ln3_b, L0_xattn_a2_li2_w, L0_xattn_a2_li2_b, L0_xattn_a2_li3_w, L0_xattn_a2_li3_b, L0_ffn_W_r, L0_ffn_W_k, L0_ffn_W_v, L0_ffn_mu_r, L0_ffn_mu_k, L1_attn_q1_w, L1_attn_k1_w, L1_attn_k2_w, L1_attn_gw_w, L1_attn_sw_w, L1_attn_c_proj_w, L1_xattn_Wq, L1_xattn_bq, L1_xattn_Wk, L1_xattn_bk, L1_xattn_Wv, L1_xattn_bv, L1_xattn_Wo, L1_xattn_bo, L1_ffn_centroids, L1_ffn_gamma, L1_ffn_beta, L1_ffn_W1, L1_ffn_b1, L1_ffn_W2, L1_ffn_b2):
    import jax
    import jax.numpy as jnp

    def _L0_attn_ref(u, W_in, b_in, W_x, b_x, W_dt, b_dt, A_log, D, W_out, b_out):
        import jax, jax.numpy as jnp
        import numpy as np
        D_MODEL = 128
        D_STATE = 16
        EXPAND = 2
        D_INNER = D_MODEL * EXPAND
        DT_RANK = D_MODEL // 16

        def _ssm_forward(u, W_in, b_in, W_x, b_x, W_dt, b_dt, A_log, D, W_out, b_out):
            B, T, _ = u.shape
            u_inner = u @ W_in.T + b_in
            x, z = jnp.split(u_inner, 2, axis=-1)
            dbc = x @ W_x.T + b_x
            delta_raw = dbc[..., :DT_RANK]
            B_ssm = dbc[..., DT_RANK:DT_RANK + D_STATE]
            C_ssm = dbc[..., DT_RANK + D_STATE:]
            delta = jax.nn.softplus(delta_raw @ W_dt.T + b_dt)
            A = -jnp.exp(A_log)

            def step(h, xs):
                dt_t, x_t, Bt, Ct = xs
                dA = jnp.exp(dt_t[..., None] * A)
                dB = dt_t[..., None] * Bt[:, None, :]
                h = h * dA + x_t[..., None] * dB
                y_t = jnp.einsum('bdn,bn->bd', h, Ct)
                return (h, y_t)
            h0 = jnp.zeros((B, D_INNER, D_STATE), u.dtype)
            xs = (jnp.swapaxes(delta, 0, 1), jnp.swapaxes(x, 0, 1), jnp.swapaxes(B_ssm, 0, 1), jnp.swapaxes(C_ssm, 0, 1))
            _, y = jax.lax.scan(step, h0, xs)
            y = jnp.swapaxes(y, 0, 1)
            y = y + x * D
            y = y * (z * jax.nn.sigmoid(z))
            return y @ W_out.T + b_out
        return _ssm_forward(u, W_in, b_in, W_x, b_x, W_dt, b_dt, A_log, D, W_out, b_out)

    def _L0_xattn_ref(xx, ee, ln1_g, ln1_b, ln2_g, ln2_b, a1_wq, a1_wk, a1_wv, a1_li1_w, a1_li1_b, a1_lnx_g, a1_lnx_b, a1_lny_g, a1_lny_b, a1_ln3_g, a1_ln3_b, a1_li2_w, a1_li2_b, a1_li3_w, a1_li3_b, a2_wq, a2_wk, a2_wv, a2_li1_w, a2_li1_b, a2_lnx_g, a2_lnx_b, a2_lny_g, a2_lny_b, a2_ln3_g, a2_ln3_b, a2_li2_w, a2_li2_b, a2_li3_w, a2_li3_b, training):
        import jax, jax.numpy as jnp
        import numpy as np
        H, D, C1, C2, S, M, B, W = (16, 32, 128, 64, 256, 64, 2, 4)

        def _ln(x, g, b):
            m = jnp.mean(x, -1, keepdims=True)
            v = jnp.var(x, -1, keepdims=True)
            return (x - m) * jax.lax.rsqrt(v + 1e-05) * g + b

        def _mha(x, y, wq, wk, wv, li1_w, li1_b, lnx_g, lnx_b, lny_g, lny_b, ln3_g, ln3_b, li2_w, li2_b, li3_w, li3_b, causal):
            xn = _ln(x, lnx_g, lnx_b)
            yn = _ln(y, lny_g, lny_b)
            q = jnp.einsum('bsc,hcd->bhsd', xn, wq)
            k = jnp.einsum('btc,hcd->bhtd', yn, wk)
            v = jnp.einsum('btc,hcd->bhtd', yn, wv)
            a = jax.nn.softmax(jnp.einsum('bhsd,bhtd->bhst', q, k) * D ** (-0.5), axis=-1)
            if causal:
                s, t = (a.shape[-2], a.shape[-1])
                mask = (jnp.arange(t)[None, :] > jnp.arange(s)[:, None]).astype(a.dtype)
                a = a * mask
            o = jnp.einsum('bhst,bhtd->bhsd', a, v)
            o = o.transpose(0, 2, 1, 3).reshape(x.shape[0], x.shape[1], H * D)
            x_out = x + o @ li1_w + li1_b
            h = jax.nn.gelu(_ln(x_out, ln3_g, ln3_b) @ li2_w + li2_b, approximate=False)
            return x_out + h @ li3_w + li3_b
        x = _ln(xx, ln1_g, ln1_b)
        x = x + _mha(x, x, a1_wq, a1_wk, a1_wv, a1_li1_w, a1_li1_b, a1_lnx_g, a1_lnx_b, a1_lny_g, a1_lny_b, a1_ln3_g, a1_ln3_b, a1_li2_w, a1_li2_b, a1_li3_w, a1_li3_b, causal=True)
        x = _ln(x, ln2_g, ln2_b)
        return x + _mha(x, ee, a2_wq, a2_wk, a2_wv, a2_li1_w, a2_li1_b, a2_lnx_g, a2_lnx_b, a2_lny_g, a2_lny_b, a2_ln3_g, a2_ln3_b, a2_li2_w, a2_li2_b, a2_li3_w, a2_li3_b, causal=False)

    def _L0_ffn_ref(x, W_r, W_k, W_v, mu_r, mu_k):
        import jax, jax.numpy as jnp
        import numpy as np
        DIM = 128

        def _reference_tuple_inner(x, W_r, W_k, W_v, mu_r, mu_k):
            B, T, C = x.shape
            x_prev = jnp.concatenate([jnp.zeros((B, 1, C), x.dtype), x[:, :-1, :]], axis=1)
            xr = mu_r * x + (1.0 - mu_r) * x_prev
            xk = mu_k * x + (1.0 - mu_k) * x_prev
            r = jax.nn.sigmoid(jnp.einsum('btc,dc->btd', xr, W_r))
            k = jnp.einsum('btc,dc->btd', xk, W_k)
            k_act = jnp.square(jax.nn.relu(k))
            out = r * jnp.einsum('btc,dc->btd', k_act, W_v)
            new_state = x[:, -1, :]
            return (out, new_state)
        return _reference_tuple_inner(x, W_r, W_k, W_v, mu_r, mu_k)[0]

    def _L1_attn_ref(X, q1_w, k1_w, k2_w, gw_w, sw_w, c_proj_w):
        import jax, jax.numpy as jnp
        import numpy as np
        import math
        B, L, D, H = (2, 128, 128, 16)
        d = D // H
        b, l, dim = X.shape
        Q = (X @ q1_w.T).reshape(b, l, H, d)
        K = (X @ k1_w.T).reshape(b, l, H, d)
        V = X.reshape(b, l, H, d)
        W = K[..., :, None] * V[..., None, :]
        G = jax.nn.sigmoid(X.reshape(b, l, H, d) @ gw_w.T)
        G = jnp.clip(G, 1e-06, None)
        Gc = jnp.exp(jnp.clip(jnp.cumsum(jnp.log(G), axis=1), -30.0, 30.0)) + 1e-06
        Gc = Gc[..., None]
        R = jax.nn.silu(K @ sw_w.T)[..., None]
        Wc = jnp.cumsum(W * R / Gc, axis=1) * Gc
        O1 = jnp.einsum('blhd,blhde->blhe', Q, Wc)
        E = V[:, 1:] - O1[:, :-1]
        sqd = math.sqrt(d)
        Qm = Q[:, :-1] * (-1.0 / sqd)
        Qm = -jnp.where(Qm >= 0, Qm, 0.02 * Qm)
        K2 = X[:, :-1] @ k2_w.T
        K2 = jax.nn.sigmoid(K2 / math.sqrt(dim) * 0.02).reshape(b, l - 1, H, d)
        W2 = jnp.cumsum(K2[..., :, None] * E[..., None, :], axis=1)
        O2 = jnp.einsum('blhd,blhde->blhe', Qm, W2)
        O2 = jnp.concatenate([jnp.zeros_like(O2[:, :1]), O2], axis=1)
        out = (O1.reshape(b, l, dim) + O2.reshape(b, l, dim)) @ c_proj_w.T
        return out

    def _L1_xattn_ref(q, k, v, Wq, bq, Wk, bk, Wv, bv, Wo, bo):
        import jax, jax.numpy as jnp
        import numpy as np
        HEADS = 16
        D_MODEL = 128
        IMG_MODEL = 64
        D_K = D_MODEL // HEADS
        B, LQ, _ = q.shape
        LKV = k.shape[1]
        qh = (q @ Wq + bq).reshape(B, LQ, HEADS, D_K).transpose(0, 2, 1, 3)
        kh = (k @ Wk + bk).reshape(B, LKV, HEADS, D_K).transpose(0, 2, 1, 3)
        vh = (v @ Wv + bv).reshape(B, LKV, HEADS, D_K).transpose(0, 2, 1, 3)
        scale = 1.0 / np.sqrt(D_K)
        scores = jnp.einsum('bhqd,bhkd->bhqk', qh, kh) * scale
        attn = jax.nn.softmax(scores, axis=-1)
        out = jnp.einsum('bhqk,bhkd->bhqd', attn, vh)
        concat = out.transpose(0, 2, 1, 3).reshape(B, LQ, D_MODEL)
        return concat @ Wo + bo

    def _L1_ffn_ref(x, centroids, gamma, beta, W1, b1, W2, b2):
        import jax, jax.numpy as jnp
        import numpy as np
        B, S, D, F, E = (1, 128, 128, 512, 8)
        EPS = 1e-05

        def _sublayer(xs, g, b, W1e, b1e, W2e, b2e):
            mu = jnp.mean(xs, axis=-1, keepdims=True)
            var = jnp.mean(jnp.square(xs - mu), axis=-1, keepdims=True)
            h = (xs - mu) * jax.lax.rsqrt(var + EPS) * g + b
            return xs + jax.nn.relu(h @ W1e.T + b1e) @ W2e.T + b2e
        feats = x.reshape(-1, x.shape[-1])
        scores = jax.lax.stop_gradient(feats @ centroids.T)
        expert = jnp.argmax(scores, axis=1)
        onehot = jax.nn.one_hot(expert, E, dtype=feats.dtype)
        alpha = jax.nn.sigmoid(jnp.sum(feats * centroids[expert], axis=-1, keepdims=True))
        ys = jax.vmap(_sublayer, in_axes=(None, 0, 0, 0, 0, 0, 0))(feats, gamma, beta, W1, b1, W2, b2)
        y = jnp.einsum('te,etd->td', onehot, ys)
        out = alpha * y + (1.0 - alpha) * feats
        return out.reshape(x.shape)
    x = _layernorm(x + _L0_attn_ref(x, L0_attn_W_in, L0_attn_b_in, L0_attn_W_x, L0_attn_b_x, L0_attn_W_dt, L0_attn_b_dt, L0_attn_A_log, L0_attn_D, L0_attn_W_out, L0_attn_b_out), axis=-1)
    x = _layernorm(x + _L0_xattn_ref(x, ctx_512, L0_xattn_ln1_g, L0_xattn_ln1_b, L0_xattn_ln2_g, L0_xattn_ln2_b, L0_xattn_a1_wq, L0_xattn_a1_wk, L0_xattn_a1_wv, L0_xattn_a1_li1_w, L0_xattn_a1_li1_b, L0_xattn_a1_lnx_g, L0_xattn_a1_lnx_b, L0_xattn_a1_lny_g, L0_xattn_a1_lny_b, L0_xattn_a1_ln3_g, L0_xattn_a1_ln3_b, L0_xattn_a1_li2_w, L0_xattn_a1_li2_b, L0_xattn_a1_li3_w, L0_xattn_a1_li3_b, L0_xattn_a2_wq, L0_xattn_a2_wk, L0_xattn_a2_wv, L0_xattn_a2_li1_w, L0_xattn_a2_li1_b, L0_xattn_a2_lnx_g, L0_xattn_a2_lnx_b, L0_xattn_a2_lny_g, L0_xattn_a2_lny_b, L0_xattn_a2_ln3_g, L0_xattn_a2_ln3_b, L0_xattn_a2_li2_w, L0_xattn_a2_li2_b, L0_xattn_a2_li3_w, L0_xattn_a2_li3_b, 0), axis=-1)
    x = _layernorm(x + _L0_ffn_ref(x, L0_ffn_W_r, L0_ffn_W_k, L0_ffn_W_v, L0_ffn_mu_r, L0_ffn_mu_k), axis=-1)
    x = _layernorm(x + _L1_attn_ref(x, L1_attn_q1_w, L1_attn_k1_w, L1_attn_k2_w, L1_attn_gw_w, L1_attn_sw_w, L1_attn_c_proj_w), axis=-1)
    x = _layernorm(x + _L1_xattn_ref(x, ctx_512, ctx_512, L1_xattn_Wq, L1_xattn_bq, L1_xattn_Wk, L1_xattn_bk, L1_xattn_Wv, L1_xattn_bv, L1_xattn_Wo, L1_xattn_bo), axis=-1)
    x = _layernorm(x + _L1_ffn_ref(x, L1_ffn_centroids, L1_ffn_gamma, L1_ffn_beta, L1_ffn_W1, L1_ffn_b1, L1_ffn_W2, L1_ffn_b2), axis=-1)
    return x

_drawn_inputs = setup_inputs


def setup_inputs(seed=0):
    import zlib

    import numpy as np

    out = dict(_drawn_inputs(seed))
    spreads = {'L0_attn_D': (1.0, 0.2),
     'L0_xattn_ln1_g': (1.0, 0.2),
     'L0_xattn_ln1_b': (0.0, 0.1),
     'L0_xattn_ln2_g': (1.0, 0.2),
     'L0_xattn_ln2_b': (0.0, 0.1),
     'L0_xattn_a1_li1_b': (0.0, 0.1),
     'L0_xattn_a1_lnx_g': (1.0, 0.6),
     'L0_xattn_a1_lnx_b': (0.0, 0.8),
     'L0_xattn_a1_lny_g': (1.0, 0.6),
     'L0_xattn_a1_lny_b': (0.0, 0.8),
     'L0_xattn_a1_ln3_g': (1.0, 0.6),
     'L0_xattn_a1_ln3_b': (0.0, 0.8),
     'L0_xattn_a1_li2_b': (0.0, 0.1),
     'L0_xattn_a1_li3_b': (0.0, 0.1),
     'L0_xattn_a2_li1_b': (0.0, 0.1),
     'L0_xattn_a2_lnx_g': (1.0, 0.6),
     'L0_xattn_a2_lnx_b': (0.0, 0.8),
     'L0_xattn_a2_lny_g': (1.0, 0.6),
     'L0_xattn_a2_lny_b': (0.0, 0.754),
     'L0_xattn_a2_ln3_g': (1.0, 0.6),
     'L0_xattn_a2_ln3_b': (0.0, 0.8),
     'L0_xattn_a2_li2_b': (0.0, 0.1),
     'L0_xattn_a2_li3_b': (0.0, 0.1),
     'L1_xattn_bq': (0.0, 0.353),
     'L1_xattn_bk': (0.0, 2.0),
     'L1_xattn_bv': (0.0, 0.1),
     'L1_xattn_bo': (0.0, 0.1),
     'L1_ffn_gamma': (1.0, 0.6),
     'L1_ffn_beta': (0.0, 2.0),
     'L1_ffn_b1': (0.0, 0.606),
     'L1_ffn_b2': (0.0, 0.1)}
    factors = {'L0_attn_W_dt': 3.201,
     'L0_attn_b_dt': 3.748,
     'L0_xattn_a1_wq': 8.0,
     'L0_xattn_a1_wk': 8.0,
     'L0_xattn_a1_wv': 3.192,
     'L0_xattn_a1_li1_w': 3.048,
     'L0_xattn_a2_wq': 8.0,
     'L0_xattn_a2_wk': 8.0,
     'L0_ffn_mu_r': 3.496,
     'L1_attn_k2_w': 64.0}
    for name, (base, spread) in spreads.items():
        noise = np.random.default_rng([zlib.crc32(name.encode()), seed]).standard_normal(out[name].shape)
        drawn = base * np.exp(spread * noise) if base else spread * noise
        out[name] = jnp.asarray(drawn.astype(out[name].dtype))
    for name, factor in factors.items():
        out[name] = (out[name] * factor).astype(out[name].dtype)
    return out
```

```python
from contextlib import ExitStack

import numpy as np

import concourse.bass as bass
from concourse import mybir

F32 = mybir.dt.float32
BF16 = mybir.dt.bfloat16
ALU = mybir.AluOpType
ACT = mybir.ActivationFunctionType
AX = mybir.AxisListType

T = 128
C = 128
P = 128
GROUP = 4
GT = GROUP * T
EPS = 1e-5




def needed(count):
    return not (isinstance(count, int) and count <= 0)


def bcast(ap, dim, n):
    shape = list(ap.shape)
    return ap.unsqueeze(dim).broadcast_to(shape[:dim] + [n] + shape[dim:])


def by_batch(ap):
    return ap.rearrange("p (b n) -> p b n", b=GROUP)


def over_groups(eng, n, step, body):
    body(0)
    if n > step:
        with eng.Fori(step, n - step + 1, step) as g:
            body(g)


class Phase:

    def __init__(self, nc, name):
        self.nc, self.name = nc, name

    def __enter__(self):
        self.stack, self.sems = ExitStack(), []
        return self

    def sb(self, name, shape, dt=F32):
        return self.stack.enter_context(self.nc.sbuf_tensor(f"{self.name}_{name}", shape, dt))

    def bank(self, name):
        return self.stack.enter_context(self.nc.psum_tensor(f"{self.name}_{name}", [P, 512], F32))

    def sem(self, name):
        s = self.nc.alloc_semaphore(name=f"{self.name}_{name}")
        self.sems.append(s)
        return s

    def block(self):
        return self.stack.enter_context(self.nc.Block())

    def __exit__(self, *_):
        self.stack.close()
        self.nc.all_engine_barrier()
        self.nc.clear_and_free_semaphores(self.sems)
        self.nc.all_engine_barrier()


class Weights:

    def __init__(self):
        self.at, self.n, self.parts = {}, 0, []

    def add(self, name, a):
        a = np.asarray(a)
        assert a.ndim == 2 and a.shape[0] <= P
        self.at[name] = (self.n, a.shape)
        self.parts.append(a)
        self.n += a.shape[1]

    def packed(self):
        out = np.zeros((P, self.n), np.float32)
        for (at, shape), a in zip(self.at.values(), self.parts):
            out[: shape[0], at : at + shape[1]] = a
        return out

    def view(self, tile, name):
        at, (rows, cols) = self.at[name]
        return tile[0:rows, at : at + cols]


def row_stats(dve, src, stats, mv, done, base, mark):
    for b in range(GROUP):
        dve.bn_stats(stats[:, b, :], src(b)).then_inc(done, 1)
    dve.wait_ge(done, base + GROUP)
    dve.sem_inc(mark, 1)
    for b in range(GROUP):
        dve.bn_aggr(mv[:, b, :], stats[:, b, :]).then_inc(done, 1)


def inv_std(pool, power, mv, rstd, done, base):
    pool.tensor_scalar(rstd, mv[:, :, 1], EPS, None, ALU.add).then_inc(done, 1)
    pool.wait_ge(done, base + 1)
    pool.tensor_tensor(rstd, rstd, power, ALU.pow).then_inc(done, 1)


def normalise(dve, dst, src, mv, rstd):
    for b in range(GROUP):
        op = dve.tensor_scalar(dst(b), src(b), mv[:, b, 0:1], rstd[:, b:b + 1], ALU.subtract, ALU.mult)
    return op




def ssm_phase(nc, env, name, wd, w):
    X, NG = env["X"], env["NG"]
    N = 16
    HT = 2 * GT
    LAGS = 6
    with Phase(nc, name) as ph:
        wt = ph.sb("wt", [P, w.n])
        V = lambda k: w.view(wt, k)
        ident, w_in, b_in, w_x, b_x, w_dt, b_dt, a_log, d_skip, w_out, bor, pick = (V(k) for k in (
            "ident", "w_in", "b_in", "w_x", "b_x", "w_dt", "b_dt", "a_log", "d_skip", "w_out", "bor", "pick"))
        RX = w_x.shape[1] // 2
        xT = ph.sb("xT", [P, 2, GT])
        xi = ph.sb("xi", [P, 2, 2, GT])
        zs = ph.sb("zs", [P, 2, 2, GT])
        dbc = ph.sb("dbc", [P, GT])
        rest = ph.sb("rest", [P, GT])
        parts = ph.sb("parts", [96, 2, GT], BF16)
        spread = ph.sb("spread", [96, 32, P], BF16)
        dtr = ph.sb("dtr", [P, 2, GT])
        spl = ph.sb("spl", [P, 2, GT])
        delta = ph.sb("delta", [P, 2, 2, GT])
        dx = ph.sb("dx", [P, 2, 2, GT])
        nega = ph.sb("nega", [P, 2 * N])
        dA = ph.sb("dA", [P, 2, HT])
        Bs = ph.sb("Bs", [P, 2, GT])
        dBx = ph.sb("dBx", [P, 2, HT])
        h = ph.sb("h", [P, HT])
        hC = ph.sb("hC", [P, 2, HT])
        yg = ph.sb("yg", [P, 2, GT])
        xr = ph.sb("xr", [P, GROUP, C])
        r = ph.sb("r", [P, GROUP, C])
        stats = ph.sb("stats", [P, GROUP, 6])
        mv = ph.sb("mv", [P, GROUP, 2])
        rstd = ph.sb("rstd", [P, GROUP])
        power = ph.sb("power", [P, GROUP])
        bp = [ph.bank(f"b{i}") for i in range(2)]
        cp = [ph.bank(f"c{i}") for i in range(2)]
        yp = [ph.bank(f"y{i}") for i in range(2)]
        pj = ph.bank("pj")
        op = ph.bank("op")
        (loaded, x_in, setup, power_set, proj_mm, proj_read, dbc_ready, split, dt_ready, dx_ready,
         spread_mm, Bs_ready, dA_ready, dBx_ready, h_ready, hC_ready, y_mm, y_step, out_mm, xr_ready, r_ready, vec,
         pool_step, x_out) = (ph.sem(k) for k in (
             "loaded", "x_in", "setup", "power_set", "proj_mm", "proj_read", "dbc_ready", "split",
             "dt_ready", "dx_ready", "spread_mm", "Bs_ready", "dA_ready", "dBx_ready", "h_ready",
             "hC_ready", "y_mm", "y_step", "out_mm", "xr_ready", "r_ready", "vec", "pool_step", "x_out"))
        xT_in = [ph.sem(f"xT_in{i}") for i in range(2)]
        PJ = 7
        DT = 4
        SPLIT = 5
        VEC = 2 * GROUP
        YS = 3
        SETUP = 4
        mark = ph.sem("mark")
        block = ph.block()

        def lagged(g, p, lag, slot):
            i = g * N + (p - lag)
            if isinstance(i, int) and not 0 <= i < NG * N:
                return None
            return i, (p - lag) % N, slot if p >= lag else 1 - slot

        def first(g):
            return isinstance(g, int) and g == 0

        def run(eng, head, step):
            for p in range(N):
                head(0, 0, p)
            step(0, 0, range(N), NG > 1)
            if NG > 2:
                with eng.Fori(1, NG - 2, 2) as g:
                    step(g, 1, range(N), True)
                    step(g + 1, 0, range(N), True)
            if NG > 1:
                step(NG - 1, 1, range(N), False)
            step(NG, 0, range(LAGS), False)


        @block.sync
        def _(sp):
            sp.dma_start(wt[:, :], wd).then_inc(loaded, 16)
            sp.dma_start(xT[:, 0, :], env["xT"][:, 0:GT]).then_inc(xT_in[0], 16)
            sp.dma_start(xT[:, 1, :], env["xT"][:, GT:2 * GT]).then_inc(xT_in[1], 16)
            sp.dma_start(X[:, :, :], env["x"]).then_inc(x_in, 16)

            def fetch(g, slot):
                sp.wait_ge(proj_mm, (g - 1) * PJ - 3)
                sp.dma_start(xT[:, slot, :], env["xT"][:, bass.ds(g * GT, GT)]).then_inc(xT_in[slot], 16)

            if NG > 2:
                with sp.Fori(2, NG - 1, 2) as g:
                    fetch(g, 0)
                    fetch(g + 1, 1)

        @block.tensor
        def _(pe):
            pe.wait_ge(loaded, 16)
            pe.wait_ge(setup, SETUP)

            def head(g, slot, p):
                if p in (4, 5, 6):
                    if p == 4:
                        pe.wait_ge(xT_in[slot], 8 * (g - slot) + 16)
                    for j in {4: (0,), 5: (1,), 6: (2, 3)}[p]:
                        if needed(g * PJ + min(j, 2)):
                            pe.wait_ge(proj_read, g * PJ + min(j, 2))
                        if j == 3:
                            if needed(g - 1):
                                pe.wait_ge(r_ready, g - 1)
                        pe.matmul((op if j == 3 else pj)[:, :], w_in[:, j * P:(j + 1) * P], xT[:, slot, :])\
                            .then_inc(proj_mm, 1)
                if p == 8:
                    pe.wait_ge(proj_read, g * PJ + 4)
                    pe.matmul(pj[0:RX, :], w_x[:, 0:RX], xi[:, slot, 0, :], start=True, stop=False)
                    pe.matmul(pj[0:RX, :], w_x[:, RX:2 * RX], xi[:, slot, 1, :], start=False, stop=True).then_inc(proj_mm, 1)
                if p in (10, 11):
                    j = p - 10
                    pe.wait_ge(proj_read, g * PJ + 5 + j)
                    pe.matmul(pj[:, :], w_dt[96:96 + 8, j * P:(j + 1) * P], dbc[96:96 + 8, :]).then_inc(proj_mm, 1)

            def step(g, slot, rng, more):
                for p in rng:
                    if now := lagged(g, p, 0, slot):
                        i, n, s = now
                        if n == 0:
                            pe.wait_ge(split, (g + 1) * SPLIT)
                        if needed(i - 1):
                            pe.wait_ge(Bs_ready, i - 1)
                        pe.matmul(bp[n % 2][:, :], spread[:, n, :], parts[:, s, :]).then_inc(spread_mm, 1)
                        if needed(i - 1):
                            pe.wait_ge(hC_ready, i - 1)
                        pe.matmul(cp[n % 2][:, :], spread[:, N + n, :], parts[:, s, :]).then_inc(spread_mm, 1)
                    if now := lagged(g, p, 1, slot):
                        i, n, s = now
                        if n == 0:
                            if needed((g if p >= 1 else g - 1) * YS):
                                pe.wait_ge(y_step, (g if p >= 1 else g - 1) * YS)
                        pe.wait_ge(hC_ready, i + 1)
                        for half in range(2):
                            mm = pe.matmul(yp[half][:, :], ident, hC[:, n % 2, half * GT:(half + 1) * GT],
                                           start=(n == 0), stop=(n == N - 1))
                        mm.then_inc(y_mm, 1)
                    if p == 2 and not first(g):
                        pe.wait_ge(y_step, g * YS)
                        for b in range(GROUP):
                            for half in range(2):
                                mm = pe.matmul(op[:, b * C:(b + 1) * C], yg[:, half, b * T:(b + 1) * T],
                                               w_out[:, half * C:(half + 1) * C], start=(half == 0), stop=(half == 1))
                        mm.then_inc(out_mm, 1)
                    if more:
                        head(g + 1, 1 - slot, p)

            run(pe, head, step)

        @block.scalar
        def _(act):
            act.wait_ge(loaded, 16)
            act.activation(nega[:, :], a_log, ACT.Exp).then_inc(setup, 1)

            def head(g, slot, p):
                at = g * PJ
                if p in (4, 5):
                    j = p - 4
                    act.wait_ge(proj_mm, at + j + 1)
                    if needed((g - 1) * YS):
                        act.wait_ge(y_step, (g - 1) * YS)
                    act.activation(xi[:, slot, j, :], pj[:, :], ACT.Identity, bias=b_in[:, j:j + 1])\
                        .then_inc(proj_read, 1)
                if p == 6:
                    for j in range(2):
                        act.wait_ge(proj_mm, at + 3 + j)
                        act.activation(zs[:, slot, j, :], (op if j else pj)[:, :], ACT.Silu, bias=b_in[:, 2 + j:3 + j])\
                            .then_inc(proj_read, 1)
                if p == 8:
                    act.wait_ge(proj_mm, at + 5)
                    if needed(g * SPLIT):
                        act.wait_ge(split, g * SPLIT)
                    act.activation(dbc[0:RX, :], pj[0:RX, :], ACT.Identity, bias=b_x[0:RX, :]).then_inc(proj_read, 1)
                if p in (10, 11):
                    j = p - 10
                    act.wait_ge(proj_mm, at + 6 + j)
                    if needed(g * DT):
                        act.wait_ge(dt_ready, g * DT)
                    act.activation(dtr[:, j, :], pj[:, :], ACT.Identity, bias=b_dt[:, j:j + 1]).then_inc(proj_read, 1)
                if p == 12:
                    act.wait_ge(proj_read, at + 7)
                    act.activation(spl[:, :, :], dtr[:, :, :], ACT.Abs).then_inc(dt_ready, 1)
                    act.wait_ge(dt_ready, g * DT + 1)
                    act.activation(spl[:, :, :], spl[:, :, :], ACT.Exp, scale=-1.0).then_inc(dt_ready, 1)
                    act.wait_ge(dt_ready, g * DT + 2)
                    act.activation(spl[:, :, :], spl[:, :, :], ACT.Ln, bias=1.0).then_inc(dt_ready, 1)

            def step(g, slot, rng, more):
                for p in rng:
                    if now := lagged(g, p, 0, slot):
                        i, n, s = now
                        act.wait_ge(spread_mm, 2 * i + 1)
                        if needed(i - 1):
                            act.wait_ge(dBx_ready, i - 1)
                        act.activation(Bs[:, n % 2, :], bp[n % 2][:, :], ACT.Copy).then_inc(Bs_ready, 1)
                        if n == 0:
                            act.wait_ge(dt_ready, (g + 1) * DT)
                        if needed(i - 1):
                            act.wait_ge(h_ready, i - 1)
                        for half in range(2):
                            o = act.activation(
                                dA[:, n % 2, half * GT:(half + 1) * GT].rearrange("p (b t) -> p b t", b=GROUP)[:, :, 1:T],
                                by_batch(delta[:, s, half, :])[:, :, 1:T], ACT.Exp,
                                scale=nega[:, half * N + n:half * N + n + 1])
                        o.then_inc(dA_ready, 1)
                    if more:
                        head(g + 1, 1 - slot, p)

            act.wait_ge(setup, SETUP)
            run(act, head, step)

        @block.vector
        def _(dve):
            dve.wait_ge(loaded, 16)
            dve.tensor_copy(spread[:, :, :], bcast(pick, 2, P)).then_inc(setup, 1)
            dve.memset(dA[:, :, :], 0.0).then_inc(setup, 1)
            dve.wait_ge(setup, 3)
            dve.tensor_scalar(nega[:, :], nega[:, :], -1.0, None, ALU.mult).then_inc(setup, 1)
            dve.wait_ge(setup, SETUP)

            def head(g, slot, p):
                if p == 13:
                    dve.wait_ge(dt_ready, g * DT + 3)
                    dve.scalar_tensor_tensor(delta[:, slot].rearrange("p a t -> p (a t)"),
                                             dtr[:, :, :].rearrange("p a t -> p (a t)"), 0.0,
                                             spl[:, :, :].rearrange("p a t -> p (a t)"), ALU.max, ALU.add)\
                        .then_inc(dt_ready, 1)

            def step(g, slot, rng, more):
                for p in rng:
                    if p == 1 and not first(g):
                        dve.wait_ge(y_mm, g * N)
                        for half in range(2):
                            o = dve.scalar_tensor_tensor(yg[:, half, :], xi[:, 1 - slot, half, :], d_skip[:, half:half + 1],
                                                         yp[half][:, :], ALU.mult, ALU.add)
                            o.then_inc(y_step, 1)
                        dve.wait_ge(y_step, g * YS - 1)
                        dve.tensor_tensor(yg[:, :, :], yg[:, :, :], zs[:, 1 - slot], ALU.mult).then_inc(y_step, 1)
                    if now := lagged(g, p, 0, slot):
                        i, n, s = now
                        dve.wait_ge(dA_ready, i + 1)
                        dve.wait_ge(dBx_ready, i + 1)
                        if needed(i):
                            dve.wait_ge(hC_ready, i)
                        dve.tensor_tensor_scan(h[:, :], dA[:, n % 2, :], dBx[:, n % 2, :], 0.0, ALU.mult, ALU.add)\
                            .then_inc(h_ready, 1)
                        dve.wait_ge(h_ready, i + 1)
                        dve.wait_ge(spread_mm, 2 * i + 2)
                        if needed(i - 1):
                            dve.wait_ge(y_mm, i - 1)
                        dve.tensor_tensor(hC[:, n % 2, :].rearrange("p (a t) -> p a t", a=2),
                                          h[:, :].rearrange("p (a t) -> p a t", a=2),
                                          bcast(cp[n % 2][:, :], 1, 2), ALU.mult).then_inc(hC_ready, 1)
                    if p == 3 and not first(g):
                        dve.wait_ge(out_mm, g)
                        dve.wait_ge(xr_ready, g)
                        dve.tensor_tensor(r[:, :, :], by_batch(op[:, :]), xr[:, :, :], ALU.add).then_inc(r_ready, 1)
                        dve.wait_ge(r_ready, g)
                        row_stats(dve, lambda b: r[:, b, :], stats[:, :, :], mv[:, :, :], vec, (g - 1) * VEC, mark)
                    if p == 4 and not first(g):
                        dve.wait_ge(pool_step, g * 2)
                        normalise(dve, lambda b: X[:, (g - 1) * GROUP + b, :], lambda b: r[:, b, :], mv[:, :, :], rstd[:, :])\
                            .then_inc(x_out, 1)
                    if more:
                        head(g + 1, 1 - slot, p)

            run(dve, head, step)

        @block.gpsimd
        def _(pool):
            pool.memset(power[:, :], -0.5).then_inc(power_set, 1)
            pool.wait_ge(power_set, 1)
            pool.wait_ge(x_in, 16)
            pool.wait_ge(loaded, 16)

            def head(g, slot, p):
                at = g * SPLIT
                if p == 9:
                    pool.wait_ge(proj_read, g * PJ + 5)
                    if needed((g - 1) * 2 * N):
                        pool.wait_ge(spread_mm, (g - 1) * 2 * N)
                    pool.sem_inc(mark, 1)
                    pool.tensor_copy(parts[:, slot, :], dbc[0:96, :]).then_inc(split, 1)
                    pool.wait_ge(split, at + 1)
                    for q in (32, 64):
                        o = pool.tensor_tensor(rest[q:q + 32, :], dbc[q:q + 32, :], parts[q:q + 32, slot, :], ALU.subtract)
                    o.then_inc(split, 1)
                    pool.wait_ge(split, at + 2)
                    pool.sem_inc(mark, 1)
                    for q in (32, 64):
                        o = pool.tensor_copy(parts[q:q + 32, slot, :], rest[q:q + 32, :])
                    o.then_inc(split, 1)
                    pool.wait_ge(split, at + 3)
                    pool.tensor_tensor(rest[64:96, :], rest[64:96, :], parts[64:96, slot, :], ALU.subtract)\
                        .then_inc(split, 1)
                    pool.wait_ge(split, at + 4)
                    pool.sem_inc(mark, 1)
                    pool.tensor_copy(parts[64:96, slot, :], rest[64:96, :]).then_inc(split, 1)
                    pool.wait_ge(split, at + 5)
                if p == 14:
                    pool.wait_ge(dt_ready, (g + 1) * DT)
                    pool.tensor_tensor(dx[:, slot], delta[:, slot], xi[:, slot], ALU.mult).then_inc(dx_ready, 1)

            def step(g, slot, rng, more):
                for p in rng:
                    if now := lagged(g, p, 0, slot):
                        i, n, s = now
                        if n == 0:
                            pool.wait_ge(dx_ready, g + 1)
                        pool.wait_ge(Bs_ready, i + 1)
                        if needed(i - 1):
                            pool.wait_ge(h_ready, i - 1)
                        pool.tensor_tensor(dBx[:, n % 2, :].rearrange("p (a t) -> p a t", a=2), dx[:, s],
                                           bcast(Bs[:, n % 2, :], 1, 2), ALU.mult).then_inc(dBx_ready, 1)
                    if p == 1 and not first(g):
                        pool.tensor_tensor(xr[:, :, :], X[:, bass.ds((g - 1) * GROUP, GROUP), :], by_batch(bor), ALU.add)\
                            .then_inc(xr_ready, 1)
                    if p == 3 and not first(g):
                        pool.wait_ge(vec, g * VEC)
                        pool.sem_inc(mark, 1)
                        inv_std(pool, power[:, :], mv[:, :, :], rstd[:, :], pool_step, (g - 1) * 2)
                    if more:
                        head(g + 1, 1 - slot, p)

            run(pool, head, step)




def attention_phase(nc, env, name, wd, w, kind):
    X, XB, XC, NG = env["X"], env["XB"], env["XC"], env["NG"]
    own, narrow = kind == "self", kind == "narrow"
    H = 16
    D = 8 if narrow else 32
    HD = H * D
    TK = T if own else env["S"]
    CK = C if own else env["CTX"]
    NT = HD // P
    SCALE = float(D) ** -0.5
    with Phase(nc, name) as ph:
        wt = ph.sb("wt", [P, w.n])
        V = lambda k: w.view(wt, k)
        ident, wq, wk, wv, wo, bor = (V(k) for k in ("ident", "wq", "wk", "wv", "wo", "bor"))
        if narrow:
            bias_q, bias_k, bias_v = ph.sb("bias_q", [P, 1]), V("bk"), V("bvr")
        else:
            gx, bx, gy, by = (V(k) for k in ("gx", "bx", "gy", "by"))
            bias_q, bias_k, bias_v = ph.sb("bias_q", [P, NT]), ph.sb("bias_k", [P, NT]), ph.sb("bias_v", [P, HD])
        xin = ph.sb("xin", [P, GROUP, C])
        xT = ph.sb("xT", [P, GT])
        qT = ph.sb("qT", [P, 2, NT, GT])
        kT = ph.sb("kT", [P, 2, NT, GROUP * TK])
        v = ph.sb("v", [P, 2, GROUP, HD])
        x1b = ph.sb("x1b", [P, 2, GROUP, C])
        stats = ph.sb("stats", [P, 3, GROUP, 6])
        mv = ph.sb("mv", [P, 3, GROUP, 2])
        rstd = ph.sb("rstd", [P, 3, GROUP])
        power = ph.sb("power", [P, GROUP])
        if not own:
            ctx_t = ph.sb("ctx_t", [P, 2, GROUP, CK])
            cT = ph.sb("cT", [P, 2 if narrow else 1, GROUP * TK])
        if narrow:
            km = ph.sb("km", [P, 2, H, TK])
        nmax = ph.sb("nmax", [P, 2, 4])
        probs = ph.sb("probs", [P, 4, 4, TK])
        pT = ph.sb("pT", [P, 2, 4, T])
        sums = ph.sb("sums", [P, 2, H])
        rsum = ph.sb("rsum", [P, H])
        o = ph.sb("o", [P, HD])
        oT = ph.sb("oT", [P, NT, T])
        y = ph.sb("y", [P, GROUP, C])
        sp_ = [ph.bank(f"scores{i}") for i in range(2)]
        tp = [ph.bank(f"probsT{i}") for i in range(2)]
        op_ = ph.bank("out")
        tailp = ph.bank("tail")
        pj = [ph.bank(f"proj{i}") for i in range(2)]
        (loaded, bias_mm, folded, power_set, scores_mm, max_ready, exp_ready, probs_turned, pT_ready,
         pv_mm, rsum_ready, o_ready, o_turned, oT_ready, out_mm, out_read, vec, pool_step, x1_normed, x1_ready, xin_ready, x1b_ready,
         proj_mm, by_act, by_dve, km_ready, xc_ready, x_out) = (ph.sem(k) for k in (
             "loaded", "bias_mm", "folded", "power_set", "scores_mm", "max_ready", "exp_ready",
             "probs_turned", "pT_ready", "pv_mm", "rsum_ready", "o_ready", "o_turned", "oT_ready", "out_mm", "out_read",
             "vec", "pool_step", "x1_normed", "x1_ready", "xin_ready", "x1b_ready", "proj_mm", "by_act", "by_dve",
             "km_ready", "xc_ready", "x_out"))

        ctx_in = [ph.sem(f"ctx_in{i}") for i in range(2)]

        jobs = [("x", 0, "act")] + ([("c", 0, "act")] if kind == "cross" else [])
        jobs += [("q", j, "act") for j in range(NT)] + [("k", j, "act") for j in range(NT)]
        jobs += [("v", b, "dve") for b in range(GROUP)]
        NJ = len(jobs)
        N_ACT = sum(e == "act" for *_, e in jobs)
        N_DVE = NJ - N_ACT
        emptied = []
        for n, (*_, e) in enumerate(jobs):
            k = sum(x == e for *_, x in jobs[:n]) + 1
            emptied.append((by_act, N_ACT, k) if e == "act" else (by_dve, N_DVE, k))
        LEAD = 4
        when = {n: LEAD + (n * (15 - LEAD)) // NJ for n in range(NJ)}
        job_of = {k: n for n, (k, i, _) in enumerate(jobs) if i == 0}

        def emptied_at(n, g):
            sem, per, k = emptied[n]
            return sem, g * per + k

        def bank_free_at(n, g):
            if n >= 2:
                return emptied_at(n - 2, g)
            return emptied_at(NJ - 1 if (NJ - 1) % 2 == n else NJ - 2, g - 1)

        mark = ph.sem("mark")
        block = ph.block()
        VEC = {"self": 4, "cross": 4, "narrow": 2}[kind] * GROUP
        POOL = {"self": 5, "cross": 4, "narrow": 2}[kind]
        QUADS = 4 * GROUP
        LAGS = 9

        def run(eng, head, step):
            head(0, 0, None)
            step(0, 0, range(QUADS), NG > 1)
            n = NG - 2
            if n > 0:
                assert n % 2 == 0
                with eng.Fori(1, NG - 2, 2) as g:
                    step(g, 1, range(QUADS), True)
                    step(g + 1, 0, range(QUADS), True)
            if NG > 1:
                step(NG - 1, (NG - 1) % 2, range(QUADS), False)
            step(NG, NG % 2, range(LAGS), False)

        def lagged(g, p, lag, slot):
            q = g * QUADS + (p - lag)
            if isinstance(q, int) and not 0 <= q < NG * QUADS:
                return None
            return q, g * GROUP + (p - lag) // 4, (p - lag) % QUADS, slot if p >= lag else 1 - slot

        def head_of(r, j):
            return 4 * r + j if narrow else 4 * j + r

        @block.sync
        def _(sp):
            sp.dma_start(wt[:, :], wd).then_inc(loaded, 16)
            if not own:
                def fetch(g, slot):
                    if needed((g - 1) * NJ):
                        sp.wait_ge(proj_mm, (g - 1) * NJ)
                    if kind == "cross":
                        sp.dma_start(ctx_t[0:TK, slot], env["ctx"][:, bass.ds(g * GROUP, GROUP), :]).then_inc(ctx_in[slot], 16)
                    else:
                        sp.dma_start(cT[0:CK, slot], env["ctxT"][:, bass.ds(g * (GROUP * TK), GROUP * TK)])\
                            .then_inc(ctx_in[slot], 16)
                fetch(0, 0)
                fetch(1, 1)
                if NG > 2:
                    with sp.Fori(2, NG - 1, 2) as g:
                        fetch(g, 0)
                        fetch(g + 1, 1)

        @block.tensor
        def _(pe):
            pe.wait_ge(loaded, 16)
            if not narrow:
                for j in range(NT):
                    pe.matmul(pj[0][:, j:j + 1], wq[:, j * P:(j + 1) * P], bx)
                    pe.matmul(pj[0][:, NT + j:NT + j + 1], wk[:, j * P:(j + 1) * P], by)
                pe.matmul(pj[1][:, 0:HD], V("by128"), wv).then_inc(bias_mm, 1)
                pe.wait_ge(folded, 6)

            def job(g, slot, n):
                what, i, _ = jobs[n]
                bank = pj[n % 2]
                free, count = bank_free_at(n, g)
                if needed(count):
                    pe.wait_ge(free, count)
                if what == "x":
                    pe.wait_ge(xin_ready, 2 * g + 1 if kind == "cross" else g + 1)
                    for b in range(GROUP):
                        mm = pe.transpose(bank[:, b * T:(b + 1) * T],
                                          xin[:, b, :], ident)
                elif what == "c":
                    pe.wait_ge(xin_ready, 2 * g + 2)
                    pe.sem_inc(mark, 1)
                    for b in range(GROUP):
                        mm = pe.transpose(bank[0:CK, b * TK:(b + 1) * TK], ctx_t[0:TK, slot, b, :], ident[0:TK, 0:TK])
                elif what == "q":
                    if i == 0:
                        pe.wait_ge(*emptied_at(job_of["x"], g))
                    mm = pe.matmul(bank[:, :], wq[:, i * P:(i + 1) * P], xT[:, :])
                elif what == "k":
                    if i == 0 and kind == "cross":
                        pe.wait_ge(*emptied_at(job_of["c"], g))
                    if i == 0 and narrow:
                        pe.wait_ge(ctx_in[slot], 8 * (g - slot) + 16)
                    src = xT[:, :] if own else cT[0:CK, slot if narrow else 0]
                    mm = pe.matmul(bank[:, 0:GROUP * TK], wk[0:CK, i * P:(i + 1) * P], src)
                else:
                    src = xT[:, i * T:(i + 1) * T] if own else \
                        cT[0:CK, slot if narrow else 0, i * TK:(i + 1) * TK]
                    mm = pe.matmul(bank[0:TK, 0:HD], src, wv[0:CK, :])
                mm.then_inc(proj_mm, 1)

            def head(g, slot, p):
                for n in range(NJ):
                    if p is None or when[n] == p:
                        job(g, slot, n)

            def step(g, slot, rng, more):
                for p in rng:
                    if now := lagged(g, p, 0, slot):
                        q, n, at, s = now
                        b, r = at // 4, at % 4
                        if at == 0:
                            pe.wait_ge(*emptied_at(NJ - 1, g))
                            pe.wait_ge(by_act, (g + 1) * N_ACT)
                        if needed(q - 1):
                            pe.wait_ge(exp_ready, q - 1)
                        if narrow:
                            if r == 0:
                                pe.wait_ge(km_ready, n + 1)
                            mm = pe.matmul(sp_[at % 2][:, 0:4 * TK], qT[:, s, 0, b * T:(b + 1) * T],
                                           km[:, b % 2, 4 * r:4 * r + 4, :])
                        else:
                            rows = slice(32 * r, 32 * r + 32)
                            for j in range(4):
                                mm = pe.matmul(sp_[at % 2][:, j * TK:(j + 1) * TK],
                                               qT[rows, s, j, b * T:(b + 1) * T],
                                               kT[rows, s, j, b * TK:(b + 1) * TK])
                        mm.then_inc(scores_mm, 1)
                    if now := lagged(g, p, 2, slot):
                        q, n, at, s = now
                        pe.wait_ge(exp_ready, q + 1)
                        if needed(q - 1):
                            pe.wait_ge(pT_ready, q - 1)
                        for j in range(4):
                            mm = pe.transpose(tp[at % 2][0:TK, j * T:(j + 1) * T], probs[:, at % 4, j, :], ident)
                        mm.then_inc(probs_turned, 1)
                    if now := lagged(g, p, 3, slot):
                        q, n, at, s = now
                        b, r = at // 4, at % 4
                        pe.wait_ge(pT_ready, q + 1)
                        if r == 0:
                            if needed(n):
                                pe.wait_ge(o_ready, n)
                        for j in range(4):
                            hd = head_of(r, j) * D
                            mm = pe.matmul(op_[:, hd:hd + D], pT[0:TK, at % 2, j, :], v[0:TK, s, b, hd:hd + D])
                        mm.then_inc(pv_mm, 1)
                    if p % 4 == 3 and (now := lagged(g, p, 7, slot)):
                        q, n, at, s = now
                        pe.wait_ge(o_ready, n + 1)
                        if needed(n):
                            pe.wait_ge(out_read, n)
                        for j in range(NT):
                            mm = pe.transpose(tailp[:, j * T:(j + 1) * T], o[:, j * P:(j + 1) * P], ident)
                        mm.then_inc(o_turned, 1)
                    if p % 4 == 0 and (now := lagged(g, p, 8, slot)):
                        q, n, at, s = now
                        pe.wait_ge(oT_ready, n + 1)
                        for j in range(NT):
                            mm = pe.matmul(tailp[:, 0:C], oT[:, j, :], wo[:, j * C:(j + 1) * C],
                                           start=(j == 0), stop=(j == NT - 1))
                        mm.then_inc(out_mm, 1)
                    if more:
                        head(g + 1, 1 - slot, p)

    
            run(pe, head, step)

        @block.scalar
        def _(act):
            act.wait_ge(loaded, 16)
            act.wait_ge(folded, 1 if narrow else 6)

            def empty(g, slot, n):
                what, i, e = jobs[n]
                if e != "act":
                    return
                bank = pj[n % 2]
                act.wait_ge(proj_mm, g * NJ + n + 1)
                if what == "x":
                    op = act.activation(xT[:, :], bank[:, :], ACT.Identity)
                elif what == "c":
                    op = act.activation(cT[0:CK, 0, :], bank[0:CK, 0:GROUP * TK], ACT.Identity)
                elif what == "q":
                    op = act.activation(qT[:, slot, i, :], bank[:, :], ACT.Identity, bias=bias_q[:, i:i + 1], scale=SCALE)
                else:
                    op = act.activation(kT[:, slot, i, :], bank[:, 0:GROUP * TK], ACT.Identity, bias=bias_k[:, i:i + 1])
                op.then_inc(by_act, 1)

            def head(g, slot, p):
                for n in range(NJ):
                    if p is None or when[n] == p:
                        empty(g, slot, n)

            def step(g, slot, rng, more):
                for p in rng:
                    if now := lagged(g, p, 0, slot):
                        q, n, at, s = now
                        b, r = at // 4, at % 4
                        act.wait_ge(max_ready, q + 1)
                        if needed(q - 3):
                            act.wait_ge(probs_turned, q - 3)
                        for j in range(4):
                            h = head_of(r, j)
                            op = act.activation(probs[:, at % 4, j, :], sp_[at % 2][:, j * TK:(j + 1) * TK], ACT.Exp,
                                                bias=nmax[:, at % 2, j:j + 1], accum_out=sums[:, b % 2, h:h + 1])
                        op.then_inc(exp_ready, 1)
                    if p % 4 == 3 and (now := lagged(g, p, 7, slot)):
                        q, n, at, s = now
                        act.wait_ge(o_turned, n + 1)
                        if needed(n):
                            act.wait_ge(out_mm, n)
                        act.activation(oT[:, :, :].rearrange("p j t -> p (j t)"), tailp[:, 0:NT * T], ACT.Identity)\
                           .then_inc(oT_ready, 1)
                    if more:
                        head(g + 1, 1 - slot, p)

            run(act, head, step)

        @block.vector
        def _(dve):
            dve.wait_ge(loaded, 16)
            if narrow:
                dve.tensor_scalar(bias_q[:, :], V("bq"), SCALE, None, ALU.mult).then_inc(folded, 1)
            else:
                dve.wait_ge(bias_mm, 1)
                dve.tensor_scalar(bias_q[:, :], pj[0][:, 0:NT], SCALE, None, ALU.mult).then_inc(folded, 1)
                dve.tensor_copy(bias_k[:, :], pj[0][:, NT:2 * NT]).then_inc(folded, 1)
                dve.tensor_copy(bias_v[:, :], pj[1][:, 0:HD]).then_inc(folded, 1)
                dve.tensor_scalar(wq, wq, gx, None, ALU.mult).then_inc(folded, 1)
                dve.tensor_scalar(wk, wk, gy, None, ALU.mult).then_inc(folded, 1)
                dve.tensor_scalar(wv, wv, gy, None, ALU.mult).then_inc(folded, 1)
                dve.wait_ge(folded, 6)

            def empty(g, slot, n):
                what, i, e = jobs[n]
                if e != "dve":
                    return
                dve.wait_ge(proj_mm, g * NJ + n + 1)
                dve.tensor_tensor(v[0:TK, slot, i, :], pj[n % 2][0:TK, 0:HD], bias_v[0:TK, :], ALU.add)\
                   .then_inc(by_dve, 1)

            def norms(g, slot, p):
                at = lambda b: g * GROUP + b
                if own and p == 0:
                    row_stats(dve, lambda b: X[:, at(b), :], stats[:, 0], mv[:, 0], vec, g * VEC, mark)
                if own and p == 1:
                    dve.wait_ge(pool_step, g * POOL + 2)
                    if needed(g):
                        dve.wait_ge(x1_ready, g)
                    normalise(dve, lambda b: y[:, b, :], lambda b: X[:, at(b), :], mv[:, 0], rstd[:, 0])\
                        .then_inc(x1_normed, 1)
                if own and p == 2:
                    dve.wait_ge(x1_ready, g + 1)
                    row_stats(dve, lambda b: XC[:, at(b), :], stats[:, 1], mv[:, 1], vec, g * VEC + 2 * GROUP, mark)
                if own and p == 3:
                    dve.wait_ge(pool_step, g * POOL + 5)
                    if needed((g - 1) * NJ + 1):
                        dve.wait_ge(proj_mm, (g - 1) * NJ + 1)
                    normalise(dve, lambda b: xin[:, b, :], lambda b: XC[:, at(b), :], mv[:, 1], rstd[:, 1])\
                        .then_inc(xin_ready, 1)
                if kind == "cross" and p == 0:
                    row_stats(dve, lambda b: XC[:, at(b), :], stats[:, 1], mv[:, 1], vec, g * VEC, mark)
                    dve.wait_ge(ctx_in[slot], 8 * (g - slot) + 16)
                    row_stats(dve, lambda b: ctx_t[0:TK, slot, b, :], stats[0:TK, 2], mv[0:TK, 2], vec, g * VEC + 2 * GROUP, mark)
                if kind == "cross" and p == 2:
                    dve.wait_ge(pool_step, g * POOL + 4)
                    if needed((g - 1) * NJ + 1):
                        dve.wait_ge(proj_mm, (g - 1) * NJ + 1)
                    normalise(dve, lambda b: xin[:, b, :], lambda b: XC[:, at(b), :], mv[:, 1], rstd[:, 1])\
                        .then_inc(xin_ready, 1)
                    normalise(dve, lambda b: ctx_t[0:TK, slot, b, :], lambda b: ctx_t[0:TK, slot, b, :],
                              mv[0:TK, 2], rstd[0:TK, 2])\
                        .then_inc(xin_ready, 1)

            def head(g, slot, p):
                for i in range(QUADS) if p is None else [p]:
                    norms(g, slot, i)
                for n in range(NJ):
                    if p is None or when[n] == p:
                        empty(g, slot, n)

            def step(g, slot, rng, more):
                for p in rng:
                    if now := lagged(g, p, 0, slot):
                        q, n, at, s = now
                        dve.wait_ge(scores_mm, q + 1)
                        dve.tensor_reduce(nmax[:, at % 2, :], sp_[at % 2][:, 0:4 * TK].rearrange("p (h t) -> p h t", h=4),
                                          AX.X, ALU.max, negate=True).then_inc(max_ready, 1)
                    if now := lagged(g, p, 2, slot):
                        q, n, at, s = now
                        dve.wait_ge(probs_turned, q + 1)
                        if needed(q - 1):
                            dve.wait_ge(pv_mm, q - 1)
                        src = tp[at % 2][0:TK, :].rearrange("p (h t) -> p h t", h=4)
                        if own:
                            op = dve.tensor_tensor(pT[0:TK, at % 2], src, bcast(V("mask"), 1, 4), ALU.mult)
                        else:
                            op = dve.tensor_copy(pT[0:TK, at % 2], src)
                        op.then_inc(pT_ready, 1)
                    if p % 4 == 2 and (now := lagged(g, p, 6, slot)):
                        q, n, at, s = now
                        b = at // 4
                        dve.wait_ge(pv_mm, q + 4)
                        if needed(n):
                            dve.wait_ge(o_turned, n)
                        dve.reciprocal(rsum[:, :], sums[:, b % 2, :]).then_inc(rsum_ready, 1)
                        dve.wait_ge(rsum_ready, n + 1)
                        dve.tensor_tensor(o[:, :].rearrange("p (h d) -> p h d", h=H),
                                          op_[:, 0:HD].rearrange("p (h d) -> p h d", h=H),
                                          bcast(rsum[:, :], 2, D), ALU.mult).then_inc(o_ready, 1)
                    if p % 4 == 0 and (now := lagged(g, p, 8, slot)):
                        q, n, at, s = now
                        b = at // 4
                        dve.wait_ge(out_mm, n + 1)
                        dve.wait_ge(x1b_ready, (g if p >= 8 else g - 1) + 1)
                        dst = y[:, b, :] if narrow else XB[:, n, :]
                        dve.tensor_tensor(dst, tailp[:, 0:C], x1b[:, s, b, :], ALU.add).then_inc(out_read, 1)
                    if narrow and p == 4 and lagged(g, p, 8, slot):
                        dve.wait_ge(out_read, g * GROUP)
                        row_stats(dve, lambda b: y[:, b, :], stats[:, 0], mv[:, 0], vec, (g - 1) * VEC, mark)
                    if narrow and p == 6 and lagged(g, p, 8, slot):
                        dve.wait_ge(pool_step, g * POOL)
                        normalise(dve, lambda b: X[:, (g - 1) * GROUP + b, :], lambda b: y[:, b, :], mv[:, 0],
                                  rstd[:, 0]).then_inc(x_out, 1)
                    if more:
                        head(g + 1, 1 - slot, p)

            run(dve, head, step)

        @block.gpsimd
        def _(pool):
            pool.memset(power[:, :], -0.5).then_inc(power_set, 1)
            pool.wait_ge(loaded, 16)
            pool.wait_ge(power_set, 1)

            def norms(g, slot, p):
                gb = bass.ds(g * GROUP, GROUP)
                if own and p == 0:
                    pool.wait_ge(vec, g * VEC + 2 * GROUP)
                    pool.sem_inc(mark, 1)
                    inv_std(pool, power[:, :], mv[:, 0], rstd[:, 0], pool_step, g * POOL)
                if own and p == 1:
                    pool.wait_ge(x1_normed, g + 1)
                    pool.tensor_tensor(y[:, :, :], y[:, :, :], by_batch(V("g1r")), ALU.mult).then_inc(pool_step, 1)
                    pool.wait_ge(pool_step, g * POOL + 3)
                    pool.sem_inc(mark, 1)
                    pool.tensor_tensor(XC[:, gb, :], y[:, :, :], by_batch(V("be1r")), ALU.add).then_inc(x1_ready, 1)
                if own and p == 2:
                    pool.wait_ge(vec, (g + 1) * VEC)
                    pool.sem_inc(mark, 1)
                    inv_std(pool, power[:, :], mv[:, 1], rstd[:, 1], pool_step, g * POOL + 3)
                if kind == "cross" and p == 0:
                    pool.wait_ge(vec, g * VEC + 2 * GROUP)
                    pool.sem_inc(mark, 1)
                    inv_std(pool, power[:, :], mv[:, 1], rstd[:, 1], pool_step, g * POOL)
                    pool.wait_ge(vec, (g + 1) * VEC)
                    pool.sem_inc(mark, 1)
                    inv_std(pool, power[0:TK, :], mv[0:TK, 2], rstd[0:TK, 2], pool_step, g * POOL + 2)
                if narrow and p == 0:
                    if needed((g - 1) * NJ + 1):
                        pool.wait_ge(proj_mm, (g - 1) * NJ + 1)
                    pool.tensor_copy(xin[:, :, :], X[:, gb, :]).then_inc(xin_ready, 1)
                if p == 4:
                    if own:
                        pool.wait_ge(x1_ready, g + 1)
                    if needed((g - 1) * GROUP):
                        pool.wait_ge(out_read, (g - 1) * GROUP)
                    pool.sem_inc(mark, 1)
                    pool.tensor_tensor(x1b[:, slot], (X if narrow else XC)[:, gb, :], by_batch(bor), ALU.add)\
                        .then_inc(x1b_ready, 1)

            def block_keys(n, slot, b):
                if needed(4 * (n - 1)):
                    pool.wait_ge(scores_mm, 4 * (n - 1))
                pool.tensor_tensor(km[:, b % 2], bcast(kT[:, slot, 0, b * TK:(b + 1) * TK], 1, H),
                                   bcast(V("heads"), 2, TK), ALU.mult).then_inc(km_ready, 1)

            def head(g, slot, p):
                for i in range(QUADS) if p is None else [p]:
                    norms(g, slot, i)

            def step(g, slot, rng, more):
                if narrow and isinstance(g, int) and g == 0:
                    pool.wait_ge(by_act, N_ACT)
                    block_keys(0, 0, 0)
                for p in rng:
                    if narrow and p % 4 == 1 and (now := lagged(g, p, 1, slot)):
                        q, n, at, s = now
                        b = at // 4 + 1
                        if b < GROUP:
                            block_keys(n + 1, slot, b)
                        elif more:
                            pool.wait_ge(by_act, (g + 2) * N_ACT)
                            block_keys(n + 1, 1 - slot, 0)
                    if not narrow and p % 4 == 0 and (now := lagged(g, p, 8, slot)):
                        q, n, at, s = now
                        pool.wait_ge(out_read, n + 1)
                        pool.tensor_tensor(XC[:, n, :], XC[:, n, :], XB[:, n, :], ALU.add).then_inc(xc_ready, 1)
                    if narrow and p == 4 and lagged(g, p, 8, slot):
                        pool.wait_ge(vec, g * VEC)
                        pool.sem_inc(mark, 1)
                        inv_std(pool, power[:, :], mv[:, 0], rstd[:, 0], pool_step, (g - 1) * POOL)
                    if more:
                        head(g + 1, 1 - slot, p)

            run(pool, head, step)




def mlp_phase(nc, env, name, wd, w, last):
    X, XB, XC, NG = env["X"], env["XB"], env["XC"], env["NG"]
    U = 2
    with Phase(nc, name) as ph:
        wt = ph.sb("wt", [P, w.n])
        V = lambda k: w.view(wt, k)
        ident, w2, b2, w3, b3r, g3, be3 = (V(k) for k in ("ident", "w2", "b2", "w3", "b3r", "g3", "be3"))
        bias2 = ph.sb("bias2", [P, 4])
        stats = ph.sb("stats", [P, U, 2, GROUP, 6])
        mv = ph.sb("mv", [P, U, 2, GROUP, 2])
        rstd = ph.sb("rstd", [P, U, 2, GROUP])
        power = ph.sb("power", [P, GROUP])
        z = ph.sb("z", [P, U, GROUP, C])
        zT = ph.sb("zT", [P, U, GT])
        h = ph.sb("h", [P, U, 4, GT])
        resid = ph.sb("resid", [P, U, GROUP, C])
        y = ph.sb("y", [P, U, GROUP, C])
        tp = [ph.bank(f"tp{u}") for u in range(U)]
        hp = [ph.bank(f"hp{i}") for i in range(4)]
        yp = [ph.bank(f"yp{u}") for u in range(U)]
        (loaded, bias_mm, folded, power_set, vec, z_ready, z_turned, zT_ready, h_mm, h_ready,
         y_mm, pool_step, resid_ready, y_ready, y_normed, out_ready) = (ph.sem(k) for k in (
             "loaded", "bias_mm", "folded", "power_set", "vec", "z_ready", "z_turned", "zT_ready", "h_mm",
             "h_ready", "y_mm", "pool_step", "resid_ready", "y_ready", "y_normed", "out_ready"))
        VEC = 4 * GROUP
        POOL = 4 if last else 5
        RES = 2 if last else 1
        mark = ph.sem("mark")
        block = ph.block()

        @block.sync
        def _(sp):
            sp.dma_start(wt[:, :], wd).then_inc(loaded, 16)

        @block.tensor
        def _(pe):
            pe.wait_ge(loaded, 16)
            for j in range(4):
                mm = pe.matmul(tp[0][:, j:j + 1], w2[:, j * P:(j + 1) * P], be3)
            mm.then_inc(bias_mm, 1)
            pe.wait_ge(folded, 2)

            def body(g):
                for u in range(U):
                    pe.wait_ge(z_ready, g + u + 1)
                    if needed(g + u - 1):
                        pe.wait_ge(zT_ready, g + u - 1)
                    for b in range(GROUP):
                        mm = pe.transpose(tp[u][:, b * T:(b + 1) * T], z[:, u, b, :], ident)
                    mm.then_inc(z_turned, 1)
                for u in range(U):
                    pe.wait_ge(zT_ready, g + u + 1)
                    for j in range(4):
                        if needed((g + u) * 4 + j - 3):
                            pe.wait_ge(h_ready, (g + u) * 4 + j - 3)
                        pe.matmul(hp[j][:, :], w2[:, j * P:(j + 1) * P], zT[:, u, :]).then_inc(h_mm, 1)
                for u in range(U):
                    pe.wait_ge(h_ready, (g + u + 1) * 4)
                    if needed(g + u - 1):
                        pe.wait_ge(y_ready, g + u - 1)
                    for b in range(GROUP):
                        for j in range(4):
                            mm = pe.matmul(yp[u][:, b * C:(b + 1) * C], h[:, u, j, b * T:(b + 1) * T],
                                           w3[:, j * C:(j + 1) * C], start=(j == 0), stop=(j == 3))
                    mm.then_inc(y_mm, 1)

            over_groups(pe, NG, U, body)

        @block.scalar
        def _(act):
            def body(g):
                for u in range(U):
                    act.wait_ge(z_turned, g + u + 1)
                    if needed((g + u - 1) * 4):
                        act.wait_ge(h_mm, (g + u - 1) * 4)
                    act.activation(zT[:, u, :], tp[u][:, :], ACT.Identity).then_inc(zT_ready, 1)
                for u in range(U):
                    if needed(g + u - 1):
                        act.wait_ge(y_mm, g + u - 1)
                    for j in range(4):
                        act.wait_ge(h_mm, (g + u) * 4 + j + 1)
                        act.activation(h[:, u, j, :], hp[j][:, :], ACT.Gelu, bias=bias2[:, j:j + 1])\
                           .then_inc(h_ready, 1)

            act.wait_ge(folded, 2)
            over_groups(act, NG, U, body)

        @block.vector
        def _(dve):
            dve.wait_ge(bias_mm, 1)
            dve.tensor_tensor(bias2[:, :], tp[0][:, 0:4], b2, ALU.add).then_inc(folded, 1)
            dve.tensor_scalar(w2, w2, g3, None, ALU.mult).then_inc(folded, 1)

            def body(g):
                base = g * VEC
                for u in range(U):
                    row_stats(dve, lambda b: XB[:, (g + u) * GROUP + b, :], stats[:, u, 0], mv[:, u, 0],
                              vec, base + u * 2 * GROUP, mark)
                for u in range(U):
                    dve.wait_ge(pool_step, g * POOL + 2 * u + 2)
                    if needed(g + u - 1):
                        dve.wait_ge(z_turned, g + u - 1)
                    normalise(dve, lambda b: z[:, u, b, :], lambda b: XB[:, (g + u) * GROUP + b, :],
                              mv[:, u, 0], rstd[:, u, 0]).then_inc(z_ready, 1)
                for u in range(U):
                    dve.wait_ge(y_mm, g + u + 1)
                    dve.wait_ge(resid_ready, g * RES + U + u + 1 if last else g + u + 1)
                    if needed(g + u - 1):
                        dve.wait_ge(y_normed if last else out_ready, g + u - 1)
                    dve.tensor_tensor(y[:, u], by_batch(yp[u][:, :]), resid[:, u], ALU.add).then_inc(y_ready, 1)
                    dve.wait_ge(y_ready, g + u + 1)
                    row_stats(dve, lambda b: y[:, u, b, :], stats[:, u, 1], mv[:, u, 1],
                              vec, base + (U + u) * 2 * GROUP, mark)
                for u in range(U):
                    dve.wait_ge(pool_step, g * POOL + 2 * U + (2 if last else 3) * u + 2)
                    normalise(dve, lambda b: X[:, (g + u) * GROUP + b, :] if last else y[:, u, b, :],
                              lambda b: y[:, u, b, :], mv[:, u, 1], rstd[:, u, 1]).then_inc(y_normed, 1)

            over_groups(dve, NG, U, body)

        @block.gpsimd
        def _(pool):
            pool.memset(power[:, :], -0.5).then_inc(power_set, 1)
            pool.wait_ge(loaded, 16)
            pool.wait_ge(power_set, 1)

            def body(g):
                for u in range(U):
                    gb = (g + u) * GROUP
                    if needed(g + u - 1):
                        pool.wait_ge(y_ready, g + u - 1)
                    pool.tensor_tensor(resid[:, u], XC[:, bass.ds(gb, GROUP), :], by_batch(b3r), ALU.add)\
                        .then_inc(resid_ready, 1)
                for u in range(U):
                    pool.wait_ge(vec, g * VEC + (u + 1) * 2 * GROUP)
                    pool.sem_inc(mark, 1)
                    inv_std(pool, power[:, :], mv[:, u, 0], rstd[:, u, 0], pool_step, g * POOL + 2 * u)
                if last:
                    for u in range(U):
                        pool.wait_ge(resid_ready, g * RES + U + u)
                        pool.tensor_tensor(resid[:, u], resid[:, u], X[:, bass.ds((g + u) * GROUP, GROUP), :],
                                           ALU.add).then_inc(resid_ready, 1)
                at = g * POOL + 2 * U
                for u in range(U):
                    pool.wait_ge(vec, g * VEC + (U + u + 1) * 2 * GROUP)
                    pool.sem_inc(mark, 1)
                    inv_std(pool, power[:, :], mv[:, u, 1], rstd[:, u, 1], pool_step, at)
                    at = at + 2
                    if not last:
                        pool.wait_ge(y_normed, g + u + 1)
                        pool.tensor_tensor(y[:, u], y[:, u], by_batch(V("g2r")), ALU.mult).then_inc(pool_step, 1)
                        at = at + 1
                        pool.wait_ge(pool_step, at)
                        pool.sem_inc(mark, 1)
                        pool.tensor_tensor(XC[:, bass.ds((g + u) * GROUP, GROUP), :], y[:, u],
                                           by_batch(V("be2r")), ALU.add).then_inc(out_ready, 1)

            over_groups(pool, NG, U, body)




def channel_mix_phase(nc, env, name, wd, w):
    X, NG = env["X"], env["NG"]
    U = 2
    with Phase(nc, name) as ph:
        wt = ph.sb("wt", [P, w.n])
        V = lambda k: w.view(wt, k)
        ident, wr, wr_prev, wk, wk_prev, wv, mu_r, mu_k = (V(k) for k in (
            "ident", "wr", "wr_prev", "wk", "wk_prev", "wv", "mu_r", "mu_k"))
        xc = ph.sb("xc", [P, U, GROUP, C])
        xT = ph.sb("xT", [P, U, GROUP, T + 1])
        r = ph.sb("r", [P, U, GT])
        k = ph.sb("k", [P, U, GT])
        k2 = ph.sb("k2", [P, U, GT])
        y = ph.sb("y", [P, U, GROUP, C])
        stats = ph.sb("stats", [P, U, GROUP, 6])
        mv = ph.sb("mv", [P, U, GROUP, 2])
        rstd = ph.sb("rstd", [P, U, GROUP])
        power = ph.sb("power", [P, GROUP])
        mix = ph.sb("mix", [P, 2])
        tp, rp, kp, op = ([ph.bank(f"{n}{u}") for u in range(U)] for n in ("turn", "r", "k", "out"))
        (loaded, power_set, folded, zeroed, xc_ready, x_turned, xT_ready, r_mm, k_mm, r_ready, k_ready, k2_ready,
         out_mm, out_read, vec, pool_step, x_out) = (ph.sem(n) for n in (
             "loaded", "power_set", "folded", "zeroed", "xc_ready", "x_turned", "xT_ready", "r_mm", "k_mm",
             "r_ready", "k_ready", "k2_ready", "out_mm", "out_read", "vec", "pool_step", "x_out"))
        VEC = 2 * GROUP + 1
        mark = ph.sem("mark")
        block = ph.block()

        @block.sync
        def _(sp):
            sp.dma_start(wt[:, :], wd).then_inc(loaded, 16)

        @block.tensor
        def _(pe):
            pe.wait_ge(folded, 6)
            pe.wait_ge(zeroed, 1)

            def body(g):
                for u in range(U):
                    pe.wait_ge(xc_ready, g + u + 1)
                    if needed(g + u - 1):
                        pe.wait_ge(xT_ready, g + u - 1)
                    for b in range(GROUP):
                        mm = pe.transpose(tp[u][:, b * T:(b + 1) * T], xc[:, u, b, :], ident)
                    mm.then_inc(x_turned, 1)
                for u in range(U):
                    pe.wait_ge(xT_ready, g + u + 1)
                    if needed(g + u - 1):
                        pe.wait_ge(k_ready, g + u - 1)
                    pe.matmul(kp[u][:, :], wk, xT[:, u, :, 1:T + 1], start=True, stop=False)
                    pe.matmul(kp[u][:, :], wk_prev, xT[:, u, :, 0:T], start=False, stop=True).then_inc(k_mm, 1)
                    if needed(g + u - 1):
                        pe.wait_ge(r_ready, g + u - 1)
                    for b in range(GROUP):
                        pe.matmul(rp[u][:, b * C:(b + 1) * C], xT[:, u, b, 1:T + 1], wr, start=True, stop=False)
                        mm = pe.matmul(rp[u][:, b * C:(b + 1) * C], xT[:, u, b, 0:T], wr_prev, start=False, stop=True)
                    mm.then_inc(r_mm, 1)
                for u in range(U):
                    pe.wait_ge(k2_ready, g + u + 1)
                    if needed(g + u - 1):
                        pe.wait_ge(out_read, g + u - 1)
                    for b in range(GROUP):
                        mm = pe.matmul(op[u][:, b * C:(b + 1) * C], k2[:, u, b * T:(b + 1) * T], wv)
                    mm.then_inc(out_mm, 1)

            over_groups(pe, NG, U, body)

        @block.scalar
        def _(act):
            act.wait_ge(zeroed, 1)

            def body(g):
                for u in range(U):
                    act.wait_ge(x_turned, g + u + 1)
                    if needed(g + u - 1):
                        act.wait_ge(r_mm, g + u - 1)
                    act.activation(xT[:, u, :, 1:T + 1], by_batch(tp[u][:, :]), ACT.Identity).then_inc(xT_ready, 1)
                for u in range(U):
                    act.wait_ge(k_mm, g + u + 1)
                    if needed(g + u - 1):
                        act.wait_ge(k2_ready, g + u - 1)
                    act.activation(k[:, u], kp[u][:, :], ACT.Relu).then_inc(k_ready, 1)
                    act.wait_ge(r_mm, g + u + 1)
                    if needed(g + u - 1):
                        act.wait_ge(out_read, g + u - 1)
                    act.activation(r[:, u], rp[u][:, :], ACT.Sigmoid).then_inc(r_ready, 1)

            over_groups(act, NG, U, body)

        @block.vector
        def _(dve):
            dve.wait_ge(loaded, 16)
            for i, mu in enumerate((mu_r, mu_k)):
                dve.tensor_scalar(mix[:, i:i + 1], mu, -1.0, 1.0, ALU.mult, ALU.add).then_inc(folded, 1)
            dve.wait_ge(folded, 2)
            for m, by in ((wr, mu_r), (wr_prev, mix[:, 0:1]), (wk, mu_k), (wk_prev, mix[:, 1:2])):
                dve.tensor_scalar(m, m, by, None, ALU.mult).then_inc(folded, 1)

            def body(g):
                for u in range(U):
                    base = (g + u) * VEC
                    dve.wait_ge(out_mm, g + u + 1)
                    dve.wait_ge(r_ready, g + u + 1)
                    if needed(g + u - 1):
                        dve.wait_ge(x_out, g + u - 1)
                    dve.tensor_tensor(y[:, u], by_batch(op[u][:, :]), by_batch(r[:, u]), ALU.mult).then_inc(out_read, 1)
                    dve.wait_ge(out_read, g + u + 1)
                    dve.tensor_tensor(y[:, u], y[:, u], xc[:, u], ALU.add).then_inc(vec, 1)
                    dve.wait_ge(vec, base + 1)
                    row_stats(dve, lambda b: y[:, u, b, :], stats[:, u], mv[:, u], vec, base + 1, mark)
                for u in range(U):
                    dve.wait_ge(pool_step, (g + u + 1) * 2)
                    normalise(dve, lambda b: X[:, (g + u) * GROUP + b, :], lambda b: y[:, u, b, :], mv[:, u],
                              rstd[:, u]).then_inc(x_out, 1)

            over_groups(dve, NG, U, body)

        @block.gpsimd
        def _(pool):
            pool.memset(power[:, :], -0.5).then_inc(power_set, 1)
            pool.memset(xT[:, :, :, 0:1], 0.0).then_inc(zeroed, 1)
            pool.wait_ge(power_set, 1)
            pool.wait_ge(loaded, 16)

            def body(g):
                for u in range(U):
                    if needed((g + u - 2) * VEC + 1):
                        pool.wait_ge(vec, (g + u - 2) * VEC + 1)
                    pool.tensor_copy(xc[:, u], X[:, bass.ds((g + u) * GROUP, GROUP), :]).then_inc(xc_ready, 1)
                for u in range(U):
                    pool.wait_ge(k_ready, g + u + 1)
                    if needed(g + u - 1):
                        pool.wait_ge(out_mm, g + u - 1)
                    pool.tensor_tensor(k2[:, u], k[:, u], k[:, u], ALU.mult).then_inc(k2_ready, 1)
                for u in range(U):
                    pool.wait_ge(vec, (g + u + 1) * VEC)
                    pool.sem_inc(mark, 1)
                    inv_std(pool, power[:, :], mv[:, u], rstd[:, u], pool_step, (g + u) * 2)

            over_groups(pool, NG, U, body)




def linear_attention_phase(nc, env, name, wd, w):
    X, NG = env["X"], env["NG"]
    H, D = 16, 8
    QUADS = 4 * GROUP
    LAG2 = 7
    BIG = 40.0
    with Phase(nc, name) as ph:
        wt = ph.sb("wt", [P, w.n])
        V = lambda k: w.view(wt, k)
        ident, wq, wk, wk2, gw, sw, wo, tri, tri0, up, heads = (V(k) for k in (
            "ident", "wq", "wk", "wk2", "gw", "sw", "wo", "tri", "tri0", "up", "heads"))
        xc = ph.sb("xc", [P, 2, GROUP, C])
        xT = ph.sb("xT", [P, GT])
        qT = ph.sb("qT", [P, 2, GT])
        qs = ph.sb("qs", [P, GT])
        qmT = ph.sb("qmT", [P, 2, GT])
        kT = ph.sb("kT", [P, 2, GT])
        k2a = ph.sb("k2a", [P, GT])
        k2T = ph.sb("k2T", [P, 2, GT])
        qh = ph.sb("qh", [P, 2, H, T])
        qmh = ph.sb("qmh", [P, 2, H, T])
        gr = ph.sb("gr", [P, 2, GROUP * H])
        ga = ph.sb("ga", [P, 2, GROUP * H])
        gc = ph.sb("gc", [P, 2, GROUP * H])
        rg = ph.sb("rg", [P, GROUP * H])
        vs = ph.sb("vs", [P, 2, GROUP * H, D])
        a1 = ph.sb("a1", [P, 2, 4, T])
        a2 = ph.sb("a2", [P, 2, 4, T])
        o1 = ph.sb("o1", [P, 2, C])
        e = ph.sb("e", [P, 2, C])
        os_ = ph.sb("os", [P, C])
        oT = ph.sb("oT", [P, T])
        y = ph.sb("y", [P, GROUP, C])
        stats = ph.sb("stats", [P, GROUP, 6])
        mv = ph.sb("mv", [P, GROUP, 2])
        rstd = ph.sb("rstd", [P, GROUP])
        power = ph.sb("power", [P, GROUP])
        s1 = [ph.bank(f"s1{i}") for i in range(2)]
        s2 = [ph.bank(f"s2{i}") for i in range(2)]
        o1p = ph.bank("o1p")
        o2p = ph.bank("o2p")
        tailp = ph.bank("tailp")
        pj = ph.bank("pj")
        (loaded, power_set, xc_ready, proj_mm, by_act, by_dve, gate_mm, gate_dve, gate_act, cum_mm, vs_ready,
         zeroed, qh_ready, qmh_ready, s1_mm, a1_ready, s2_mm, a2_ready, o1_mm, o1_ready, e_ready, o2_mm, os_ready,
         os_turned, oT_ready, out_mm, out_read, vec, pool_step, x_out) = (ph.sem(n) for n in (
             "loaded", "power_set", "xc_ready", "proj_mm", "by_act", "by_dve", "gate_mm", "gate_dve", "gate_act",
             "cum_mm", "vs_ready", "zeroed", "qh_ready", "qmh_ready", "s1_mm", "a1_ready", "s2_mm", "a2_ready",
             "o1_mm", "o1_ready", "e_ready", "o2_mm", "os_ready", "os_turned", "oT_ready", "out_mm", "out_read",
             "vec", "pool_step", "x_out"))
        VEC = 2 * GROUP
        ACT_N, DVE_N, GD, GA = 7, 2, 8, 4
        mark = ph.sem("mark")
        block = ph.block()

        def lagged(g, p, lag, slot):
            q = g * QUADS + (p - lag)
            if isinstance(q, int) and not 0 <= q < NG * QUADS:
                return None
            return q, g * GROUP + (p - lag) // 4, (p - lag) % QUADS, slot if p >= lag else 1 - slot

        def run(eng, head, step):
            for p in range(QUADS):
                head(0, 0, p)
            step(0, 0, range(QUADS), NG > 1)
            if NG > 2:
                with eng.Fori(1, NG - 2, 2) as g:
                    step(g, 1, range(QUADS), True)
                    step(g + 1, 0, range(QUADS), True)
            if NG > 1:
                step(NG - 1, 1, range(QUADS), False)
            step(NG, 0, range(QUADS), False)


        @block.sync
        def _(sp):
            sp.dma_start(wt[:, :], wd).then_inc(loaded, 16)

        @block.tensor
        def _(pe):
            pe.wait_ge(loaded, 16)

            def head(g, slot, p):
                if p == 1:
                    pe.wait_ge(xc_ready, g + 1)
                    if needed(g):
                        pe.wait_ge(vs_ready, g)
                    for b in range(GROUP):
                        mm = pe.transpose(pj[:, b * T:(b + 1) * T], xc[:, slot, b, :], ident)
                    mm.then_inc(proj_mm, 1)
                if p == 2:
                    pe.wait_ge(by_act, g * ACT_N + 1)
                    pe.matmul(pj[:, :], wk, xT[:, :]).then_inc(proj_mm, 1)
                if p == 4:
                    pe.wait_ge(by_act, g * ACT_N + 2)
                    pe.matmul(pj[:, :], wk2, xT[:, :]).then_inc(proj_mm, 1)
                if p == 8:
                    pe.wait_ge(by_dve, g * DVE_N + 1)
                    pe.matmul(pj[:, :], wq, xT[:, :]).then_inc(proj_mm, 1)
                if p == 10:
                    pe.wait_ge(by_act, g * ACT_N + 7)
                    n = GROUP * H
                    for b in range(GROUP):
                        pe.matmul(pj[:, b * H:(b + 1) * H], xT[:, b * T:(b + 1) * T], gw)
                        mm = pe.matmul(pj[:, n + b * H:n + (b + 1) * H], kT[:, slot, b * T:(b + 1) * T], sw)
                    mm.then_inc(gate_mm, 1)
                if p == 12:
                    pe.wait_ge(gate_dve, g * GD + 3)
                    pe.matmul(pj[:, 256:256 + GROUP * H], tri, ga[:, 0, :]).then_inc(cum_mm, 1)

            def step(g, slot, rng, more):
                for p in rng:
                    if now := lagged(g, p, 0, slot):
                        q, n, at, s = now
                        b, r = at // 4, at % 4
                        pe.wait_ge(qh_ready, n + 1)
                        if needed(q - 1):
                            pe.wait_ge(a1_ready, q - 1)
                        pe.matmul(s1[at % 2][:, :], kT[:, s, b * T:(b + 1) * T], qh[:, b % 2, 4 * r:4 * r + 4, :])\
                            .then_inc(s1_mm, 1)
                    if now := lagged(g, p, LAG2, slot):
                        q, n, at, s = now
                        b, r = at // 4, at % 4
                        pe.wait_ge(qmh_ready, n + 1)
                        if needed(q - 1):
                            pe.wait_ge(a2_ready, q - 1)
                        pe.matmul(s2[at % 2][:, :], k2T[:, s, b * T:(b + 1) * T], qmh[:, b % 2, 4 * r:4 * r + 4, :])\
                            .then_inc(s2_mm, 1)
                    if now := lagged(g, p, 1, slot):
                        q, n, at, s = now
                        b, r = at // 4, at % 4
                        if r == 0:
                            if needed(n):
                                pe.wait_ge(e_ready, n)
                            pe.wait_ge(vs_ready, (g if p >= 1 else g - 1) + 1)
                            pe.matmul(o1p[:, C:2 * C], up, xc[:, s, b, :])
                        pe.wait_ge(a1_ready, q + 1)
                        for j in range(4):
                            h = 4 * r + j
                            mm = pe.matmul(o1p[:, h * D:(h + 1) * D], a1[:, at % 2, j, :], vs[:, s, b * H + h, :])
                        mm.then_inc(o1_mm, 1)
                    if now := lagged(g, p, LAG2 + 1, slot):
                        q, n, at, s = now
                        b, r = at // 4, at % 4
                        if r == 0:
                            if needed(n):
                                pe.wait_ge(os_ready, n)
                            pe.wait_ge(e_ready, n + 1)
                        pe.wait_ge(a2_ready, q + 1)
                        for j in range(4):
                            h = 4 * r + j
                            mm = pe.matmul(o2p[:, h * D:(h + 1) * D], a2[:, at % 2, j, :], e[:, b % 2, h * D:(h + 1) * D])
                        mm.then_inc(o2_mm, 1)
                    if (p - LAG2 - 5) % 4 == 0 and (now := lagged(g, p, LAG2 + 5, slot)):
                        q, n, at, s = now
                        pe.wait_ge(os_ready, n + 1)
                        if needed(n):
                            pe.wait_ge(out_read, n)
                        pe.transpose(tailp[:, 0:T], os_[:, :], ident).then_inc(os_turned, 1)
                    if (p - LAG2 - 6) % 4 == 0 and (now := lagged(g, p, LAG2 + 6, slot)):
                        q, n, at, s = now
                        pe.wait_ge(oT_ready, n + 1)
                        pe.matmul(tailp[:, 0:C], oT[:, :], wo).then_inc(out_mm, 1)
                    if more:
                        head(g + 1, 1 - slot, p)

            run(pe, head, step)

        @block.scalar
        def _(act):
            act.wait_ge(loaded, 16)

            def head(g, slot, p):
                N = g * ACT_N
                if p == 1:
                    act.wait_ge(proj_mm, g * 4 + 1)
                    if needed(g):
                        act.wait_ge(gate_mm, g)
                    act.activation(xT[:, :], pj[:, :], ACT.Identity).then_inc(by_act, 1)
                if p == 2:
                    act.wait_ge(proj_mm, g * 4 + 2)
                    act.activation(kT[:, slot, :], pj[:, :], ACT.Identity).then_inc(by_act, 1)
                if p == 7:
                    act.wait_ge(by_dve, g * DVE_N + 1)
                    act.activation(k2a[:, :], k2a[:, :], ACT.Exp).then_inc(by_act, 1)
                    act.wait_ge(by_act, N + 3)
                    act.activation(k2a[:, :], k2a[:, :], ACT.Ln, bias=1.0).then_inc(by_act, 1)
                if p == 8:
                    act.wait_ge(by_act, N + 4)
                    if needed((g - 1) * QUADS):
                        act.wait_ge(s2_mm, (g - 1) * QUADS)
                    act.activation(k2T[:, slot, :], k2a[:, :], ACT.Exp, scale=-1.0).then_inc(by_act, 1)
                    act.wait_ge(proj_mm, g * 4 + 4)
                    act.activation(qT[:, slot, :], pj[:, :], ACT.Identity).then_inc(by_act, 1)
                    if needed(g * DVE_N):
                        act.wait_ge(by_dve, g * DVE_N)
                    act.activation(qs[:, :], pj[:, :], ACT.Copy, scale=0.02 / float(np.sqrt(D))).then_inc(by_act, 1)
                if p == 10:
                    act.wait_ge(gate_dve, g * GD + 2)
                    act.activation(ga[:, :, :], ga[:, :, :], ACT.Exp).then_inc(gate_act, 1)
                    act.wait_ge(gate_act, g * GA + 1)
                    act.activation(ga[:, :, :], ga[:, :, :], ACT.Ln, bias=1.0).then_inc(gate_act, 1)
                    act.wait_ge(gate_act, g * GA + 2)
                    act.activation(ga[:, 1, :], ga[:, 1, :], ACT.Exp, scale=-1.0).then_inc(gate_act, 1)
                if p == 12:
                    act.wait_ge(gate_dve, g * GD + 5)
                    act.activation(gc[:, slot, :], gc[:, slot, :], ACT.Exp).then_inc(gate_act, 1)

            def step(g, slot, rng, more):
                for p in rng:
                    if (p - LAG2 - 5) % 4 == 0 and (now := lagged(g, p, LAG2 + 5, slot)):
                        q, n, at, s = now
                        act.wait_ge(os_turned, n + 1)
                        if needed(n):
                            act.wait_ge(out_mm, n)
                        act.activation(oT[:, :], tailp[:, 0:T], ACT.Identity).then_inc(oT_ready, 1)
                    if more:
                        head(g + 1, 1 - slot, p)

            run(act, head, step)

        @block.vector
        def _(dve):
            dve.wait_ge(loaded, 16)

            def head(g, slot, p):
                N = g * GD
                if p == 5:
                    dve.wait_ge(proj_mm, g * 4 + 3)
                    if needed((g - 1) * ACT_N + 5):
                        dve.wait_ge(by_act, (g - 1) * ACT_N + 5)
                    dve.tensor_scalar(k2a[:, :], pj[:, :], -0.02 / float(np.sqrt(C)), BIG, ALU.mult, ALU.min)\
                        .then_inc(by_dve, 1)
                if p == 9:
                    dve.wait_ge(by_act, g * ACT_N + 7)
                    dve.scalar_tensor_tensor(qmT[:, slot, :], qT[:, slot, :], 1.0 / float(np.sqrt(D)), qs[:, :],
                                             ALU.mult, ALU.min).then_inc(by_dve, 1)
                if p == 10:
                    n = 2 * GROUP * H
                    dve.wait_ge(gate_mm, g + 1)
                    if needed(g):
                        dve.wait_ge(vs_ready, g)
                    src = pj[:, 0:n].rearrange("p (k n) -> p k n", k=2)
                    dve.tensor_scalar(ga[:, :, :], src, -1.0, BIG, ALU.mult, ALU.min).then_inc(gate_dve, 1)
                    dve.tensor_copy(gr[:, :, :], src).then_inc(gate_dve, 1)
                if p == 11:
                    dve.wait_ge(gate_act, g * GA + 3)
                    dve.tensor_scalar(ga[:, 0, :], ga[:, 0, :], -1.0, float(np.log(1e-6)), ALU.mult, ALU.max)\
                        .then_inc(gate_dve, 1)
                    dve.tensor_tensor(gr[:, 1, :], gr[:, 1, :], ga[:, 1, :], ALU.mult).then_inc(gate_dve, 1)
                if p == 12:
                    dve.wait_ge(cum_mm, g + 1)
                    dve.tensor_scalar(gc[:, slot, :], pj[:, 256:256 + GROUP * H], -30.0, 30.0, ALU.max, ALU.min)\
                        .then_inc(gate_dve, 1)
                if p == 13:
                    dve.wait_ge(gate_act, g * GA + 4)
                    dve.tensor_scalar(gc[:, slot, :], gc[:, slot, :], 1e-6, None, ALU.add).then_inc(gate_dve, 1)
                    dve.wait_ge(gate_dve, N + 6)
                    dve.reciprocal(rg[:, :], gc[:, slot, :]).then_inc(gate_dve, 1)
                    dve.wait_ge(gate_dve, N + 7)
                    dve.tensor_tensor(rg[:, :], rg[:, :], gr[:, 1, :], ALU.mult).then_inc(gate_dve, 1)

            def step(g, slot, rng, more):
                for p in rng:
                    if now := lagged(g, p, 0, slot):
                        q, n, at, s = now
                        dve.wait_ge(s1_mm, q + 1)
                        if needed(q - 1):
                            dve.wait_ge(o1_mm, q - 1)
                        dve.tensor_tensor(a1[:, at % 2], s1[at % 2][:, :].rearrange("p (h t) -> p h t", h=4),
                                          bcast(tri, 1, 4), ALU.mult).then_inc(a1_ready, 1)
                    if now := lagged(g, p, LAG2, slot):
                        q, n, at, s = now
                        dve.wait_ge(s2_mm, q + 1)
                        if needed(q - 1):
                            dve.wait_ge(o2_mm, q - 1)
                        dve.tensor_tensor(a2[:, at % 2], s2[at % 2][:, :].rearrange("p (h t) -> p h t", h=4),
                                          bcast(tri0, 1, 4), ALU.mult).then_inc(a2_ready, 1)
                    if (p - 5) % 4 == 0 and (now := lagged(g, p, 5, slot)):
                        q, n, at, s = now
                        b = at // 4
                        dve.wait_ge(o1_mm, q + 4)
                        if needed(n - 1):
                            dve.wait_ge(os_ready, n - 1)
                        dve.tensor_tensor(o1[:, b % 2].rearrange("p (h d) -> p h d", h=H),
                                          o1p[:, 0:C].rearrange("p (h d) -> p h d", h=H),
                                          bcast(gc[:, s, b * H:(b + 1) * H], 2, D), ALU.mult).then_inc(o1_ready, 1)
                        dve.wait_ge(o1_ready, n + 1)
                        if needed(q - 4):
                            dve.wait_ge(o2_mm, q - 4)
                        dve.tensor_tensor(e[:, b % 2], o1p[:, C:2 * C], o1[:, b % 2], ALU.subtract).then_inc(e_ready, 1)
                    if (p - LAG2 - 5) % 4 == 0 and (now := lagged(g, p, LAG2 + 5, slot)):
                        q, n, at, s = now
                        dve.wait_ge(o2_mm, q + 4)
                        if needed(n):
                            dve.wait_ge(os_turned, n)
                        dve.tensor_tensor(os_[:, :], o2p[:, 0:C], o1[:, (at // 4) % 2], ALU.add).then_inc(os_ready, 1)
                    if (p - LAG2 - 7) % 4 == 0 and (now := lagged(g, p, LAG2 + 7, slot)):
                        q, n, at, s = now
                        b = at // 4
                        dve.wait_ge(out_mm, n + 1)
                        dve.tensor_tensor(y[:, b, :], tailp[:, 0:C], X[:, n, :], ALU.add).then_inc(out_read, 1)
                    if p == LAG2 + 19 - QUADS and lagged(g, p, LAG2 + 19, slot):
                        dve.wait_ge(out_read, g * GROUP)
                        row_stats(dve, lambda b: y[:, b, :], stats[:, :, :], mv[:, :, :], vec, (g - 1) * VEC, mark)
                    if p == LAG2 + 21 - QUADS and lagged(g, p, LAG2 + 21, slot):
                        dve.wait_ge(pool_step, g * 2)
                        normalise(dve, lambda b: X[:, (g - 1) * GROUP + b, :], lambda b: y[:, b, :], mv[:, :, :], rstd[:, :])\
                            .then_inc(x_out, 1)
                    if more:
                        head(g + 1, 1 - slot, p)

            run(dve, head, step)

        @block.gpsimd
        def _(pool):
            pool.memset(power[:, :], -0.5).then_inc(power_set, 1)
            pool.memset(qmh[:, :, :, 0:1], 0.0).then_inc(zeroed, 1)
            pool.wait_ge(loaded, 16)
            pool.wait_ge(power_set, 1)
            pool.wait_ge(zeroed, 1)

            def by_head(n, b, slot):
                if needed(4 * (n - 1)):
                    pool.wait_ge(s1_mm, 4 * (n - 1))
                pool.tensor_tensor(qh[:, b % 2], bcast(qT[:, slot, b * T:(b + 1) * T], 1, H), bcast(heads, 2, T),
                                   ALU.mult).then_inc(qh_ready, 1)

            def by_head2(n, b, slot):
                if needed(4 * (n - 1)):
                    pool.wait_ge(s2_mm, 4 * (n - 1))
                pool.tensor_tensor(qmh[:, b % 2, :, 1:T], bcast(qmT[:, slot, b * T:(b + 1) * T - 1], 1, H),
                                   bcast(heads, 2, T - 1), ALU.mult).then_inc(qmh_ready, 1)

            def head(g, slot, p):
                if p == 0:
                    if needed((g - 1) * QUADS):
                        pool.wait_ge(o1_mm, (g - 1) * QUADS)
                    pool.tensor_copy(xc[:, slot], X[:, bass.ds(g * GROUP, GROUP), :]).then_inc(xc_ready, 1)
                if p == 14:
                    pool.wait_ge(gate_dve, (g + 1) * GD)
                    pool.tensor_tensor(vs[:, slot], xc[:, slot].rearrange("p b (h d) -> p (b h) d", d=D),
                                       bcast(rg[:, :], 2, D), ALU.mult).then_inc(vs_ready, 1)

            def step(g, slot, rng, more):
                if isinstance(g, int) and g == 0:
                    pool.wait_ge(by_act, ACT_N)
                    by_head(0, 0, 0)
                for p in rng:
                    if (p - LAG2 + 1) % 4 == 0 and (now := lagged(g, p, LAG2 - 1, slot)):
                        q, n, at, s = now
                        if at == 0:
                            pool.wait_ge(by_dve, ((g if p >= LAG2 - 1 else g - 1) + 1) * DVE_N)
                        by_head2(n, at // 4, s)
                    if p % 4 == 1 and (now := lagged(g, p, 1, slot)):
                        q, n, at, s = now
                        b = at // 4 + 1
                        if b < GROUP:
                            by_head(n + 1, b, slot)
                        elif more:
                            pool.wait_ge(by_act, (g + 2) * ACT_N)
                            by_head(n + 1, 0, 1 - slot)
                    if p == LAG2 + 19 - QUADS and lagged(g, p, LAG2 + 19, slot):
                        pool.wait_ge(vec, g * VEC)
                        pool.sem_inc(mark, 1)
                        inv_std(pool, power[:, :], mv[:, :, :], rstd[:, :], pool_step, (g - 1) * 2)
                    if more:
                        head(g + 1, 1 - slot, p)

            run(pool, head, step)




def experts_phase(nc, env, name, wd, w, out):
    X, NG, E = env["X"], env["NG"], env["E"]
    NF = 4
    F = NF * P
    with Phase(nc, name) as ph:
        wt = ph.sb("wt", [P, w.n])
        V = lambda k: w.view(wt, k)
        ident, cen, gamma, beta, w1, b1, w2, b2, rank = (V(k) for k in (
            "ident", "cen", "gamma", "beta", "w1", "b1", "w2", "b2", "rank"))
        bias1 = ph.sb("bias1", [P, E * NF])
        xc = ph.sb("xc", [P, 2, GROUP, C])
        z = ph.sb("z", [P, GROUP, C])
        xT = ph.sb("xT", [P, GT])
        zT = ph.sb("zT", [P, 2, GT])
        score = ph.sb("score", [P, GROUP, E])
        best = ph.sb("best", [P, GROUP])
        key = ph.sb("key", [P, GROUP, E])
        kbest = ph.sb("kbest", [P, GROUP])
        alpha = ph.sb("alpha", [P, GROUP])
        gate = ph.sb("gate", [P, 2, GROUP, E])
        gateT = ph.sb("gateT", [P, GT])
        hid = ph.sb("hid", [P, 2, NF, GT])
        acc = ph.sb("acc", [P, 2, GROUP, C])
        res = ph.sb("res", [P, 2, GROUP, C])
        stats = ph.sb("stats", [P, 2, GROUP, 6])
        mv = ph.sb("mv", [P, 2, GROUP, 2])
        rstd = ph.sb("rstd", [P, 2, GROUP])
        power = ph.sb("power", [P, GROUP])
        hp = [ph.bank(f"hid{i}") for i in range(4)]
        yp = [ph.bank(f"out{i}") for i in range(2)]
        mp = [ph.bank(f"misc{i}") for i in range(2)]
        (loaded, bias_mm, folded, power_set, xc_ready, vec, pool_step, z_ready, turned, xT_ready, zT_ready,
         score_mm, gate_step, alpha_in, alpha_exp, gate_ready, gate_turned, gateT_ready, b2_mm, acc_ready,
         hid_mm, hid_act, hid_dve, y_mm, y_read, res_ready) = (ph.sem(n) for n in (
             "loaded", "bias_mm", "folded", "power_set", "xc_ready", "vec", "pool_step", "z_ready", "turned",
             "xT_ready", "zT_ready", "score_mm", "gate_step", "alpha_in", "alpha_exp", "gate_ready",
             "gate_turned", "gateT_ready", "b2_mm", "acc_ready", "hid_mm", "hid_act", "hid_dve", "y_mm",
             "y_read", "res_ready"))
        stored = [ph.sem(f"stored{i}") for i in range(2)]
        VEC = 4 * GROUP
        GS = 5
        mark = ph.sem("mark")
        block = ph.block()

        RELU = ["act", "dve", "act", "act"]
        A = sum(e == "act" for e in RELU)
        D = NF - A

        def hid_done(eng, i):
            eng.wait_ge(hid_act, (i + 1) * A)
            eng.wait_ge(hid_dve, (i + 1) * D)

        def run(head, step, tail):
            def go(eng):
                head(0, 0)
                step(0, 0, NG > 1)
                if NG > 2:
                    with eng.Fori(1, NG - 2, 2) as g:
                        step(g, 1, True)
                        step(g + 1, 0, True)
                if NG > 1:
                    step(NG - 1, 1, False)
                tail(NG - 1, 1)
            return go

        def vec_at(g, part):
            return _order(g, part) * 2 * GROUP

        def pool_at(g, part):
            return _order(g, part) * 2

        def _order(g, part):
            if part == 0:
                return 0 if isinstance(g, int) and g == 0 else 2 * g - 1
            if isinstance(g, int) and g == NG - 1:
                return 2 * NG - 1
            return 2 * g + 2

        @block.sync
        def _(sp):
            sp.dma_start(wt[:, :], wd).then_inc(loaded, 16)
            for u in range(2):
                sp.sem_inc(stored[u], 16)

            def body(g):
                for u in range(2):
                    sp.wait_ge(res_ready, g + u + 1)
                    sp.dma_start(out[:, bass.ds((g + u) * GROUP, GROUP), :], res[:, u]).then_inc(stored[u], 16)

            over_groups(sp, NG, 2, body)
            for u in range(2):
                sp.wait_ge(stored[u], 16 + 8 * NG)

        @block.tensor
        def _(pe):
            pe.wait_ge(loaded, 16)
            for e in range(E):
                for j in range(NF):
                    mm = pe.matmul(mp[0][:, e * NF + j:e * NF + j + 1], w1[:, e * F + j * P:e * F + (j + 1) * P],
                                   beta[:, e:e + 1])
            mm.then_inc(bias_mm, 1)
            pe.wait_ge(folded, 1 + E)

            def head_part(g, slot, e):
                if e == 1:
                    pe.wait_ge(xc_ready, g + 1)
                    if needed(g):
                        pe.wait_ge(gateT_ready, g)
                    for b in range(GROUP):
                        mm = pe.transpose(mp[0][:, b * T:(b + 1) * T], xc[:, slot, b, :], ident)
                    mm.then_inc(turned, 1)
                if e == 2:
                    pe.wait_ge(z_ready, g + 1)
                    if needed(g):
                        pe.wait_ge(acc_ready, g)
                    for b in range(GROUP):
                        mm = pe.transpose(mp[1][:, b * T:(b + 1) * T], z[:, b, :], ident)
                    mm.then_inc(turned, 1)
                    pe.wait_ge(xT_ready, g + 1)
                    for b in range(GROUP):
                        mm = pe.matmul(mp[0][:, b * E:(b + 1) * E], xT[:, b * T:(b + 1) * T], cen)
                    mm.then_inc(score_mm, 1)
                if e == 5:
                    pe.wait_ge(gate_ready, g + 1)
                    for b in range(GROUP):
                        mm = pe.transpose(mp[0][0:E, b * T:(b + 1) * T], gate[:, slot, b, :], ident)
                    mm.then_inc(gate_turned, 1)
                if e == 6:
                    pe.wait_ge(gateT_ready, g + 1)
                    pe.wait_ge(zT_ready, g + 1)
                    for b in range(GROUP):
                        mm = pe.matmul(mp[1][:, b * C:(b + 1) * C], gateT[0:E, b * T:(b + 1) * T], b2)
                    mm.then_inc(b2_mm, 1)

            def second(i, k):
                hid_done(pe, i)
                if needed(i - 1):
                    pe.wait_ge(y_read, i - 1)
                for b in range(GROUP):
                    for j in range(NF):
                        mm = pe.matmul(yp[k % 2][:, b * C:(b + 1) * C], hid[:, k % 2, j, b * T:(b + 1) * T],
                                       w2[:, (k * NF + j) * C:(k * NF + j + 1) * C], start=(j == 0), stop=(j == NF - 1))
                mm.then_inc(y_mm, 1)

            def head(g, slot):
                for e in range(E):
                    head_part(g, slot, e)

            def step(g, slot, more):
                pe.wait_ge(zT_ready, g + 1)
                for e in range(E):
                    i = g * E + e
                    for j in range(NF):
                        if RELU[j] == "act":
                            if needed((i - 1) * A + sum(x == "act" for x in RELU[:j + 1])):
                                pe.wait_ge(hid_act, (i - 1) * A + sum(x == "act" for x in RELU[:j + 1]))
                        else:
                            if needed((i - 1) * D + sum(x == "dve" for x in RELU[:j + 1])):
                                pe.wait_ge(hid_dve, (i - 1) * D + sum(x == "dve" for x in RELU[:j + 1]))
                        pe.matmul(hp[j][:, :], w1[:, e * F + j * P:e * F + (j + 1) * P], zT[:, slot, :])\
                            .then_inc(hid_mm, 1)
                    if e or not (isinstance(g, int) and g == 0):
                        second(i - 1, (e - 1) % E)
                    if more:
                        head_part(g + 1, 1 - slot, e)

            def tail(g, slot):
                second(g * E + E - 1, E - 1)

            run(head, step, tail)(pe)

        @block.scalar
        def _(act):
            act.wait_ge(folded, 1 + E)

            def head_part(g, slot, e):
                if e == 1:
                    act.wait_ge(turned, 2 * g + 1)
                    if needed(g):
                        act.wait_ge(score_mm, g)
                    act.activation(xT[:, :], mp[0][:, :], ACT.Identity).then_inc(xT_ready, 1)
                if e == 2:
                    act.wait_ge(turned, 2 * g + 2)
                    act.activation(zT[:, slot, :], mp[1][:, :], ACT.Identity).then_inc(zT_ready, 1)
                if e == 4:
                    act.wait_ge(alpha_in, g + 1)
                    act.activation(alpha[:, :], best[:, :], ACT.Sigmoid).then_inc(alpha_exp, 1)
                if e == 5:
                    act.wait_ge(gate_turned, g + 1)
                    if needed(g):
                        act.wait_ge(b2_mm, g)
                    act.activation(gateT[0:E, :], mp[0][0:E, :], ACT.Identity).then_inc(gateT_ready, 1)

            def head(g, slot):
                for e in range(E):
                    head_part(g, slot, e)

            def step(g, slot, more):
                for e in range(E):
                    i = g * E + e
                    if needed(i - 1):
                        act.wait_ge(y_mm, i - 1)
                    for j in range(NF):
                        if RELU[j] == "act":
                            act.wait_ge(hid_mm, i * NF + j + 1)
                            act.activation(hid[:, e % 2, j, :], hp[j][:, :], ACT.Relu,
                                           bias=bias1[:, e * NF + j:e * NF + j + 1]).then_inc(hid_act, 1)
                    if more:
                        head_part(g + 1, 1 - slot, e)

            run(head, step, lambda g, slot: None)(act)

        @block.vector
        def _(dve):
            dve.wait_ge(bias_mm, 1)
            dve.tensor_tensor(bias1[:, :], mp[0][:, 0:E * NF], b1, ALU.add).then_inc(folded, 1)
            for e in range(E):
                dve.tensor_scalar(w1[:, e * F:(e + 1) * F], w1[:, e * F:(e + 1) * F], gamma[:, e:e + 1], None, ALU.mult)\
                    .then_inc(folded, 1)

            def head_part(g, slot, e):
                at = g * GS
                if e == 0:
                    dve.wait_ge(xc_ready, g + 1)
                    row_stats(dve, lambda b: xc[:, slot, b, :], stats[:, 0], mv[:, 0], vec,
                              vec_at(g, 0), mark)
                if e == 1:
                    dve.wait_ge(pool_step, pool_at(g, 0) + 2)
                    if needed(2 * g):
                        dve.wait_ge(turned, 2 * g)
                    normalise(dve, lambda b: z[:, b, :], lambda b: xc[:, slot, b, :], mv[:, 0], rstd[:, 0])\
                        .then_inc(z_ready, 1)
                if e == 3:
                    dve.wait_ge(score_mm, g + 1)
                    if needed(g):
                        dve.wait_ge(gate_ready, g)
                    dve.tensor_copy(score[:, :, :], mp[0][:, 0:GROUP * E].rearrange("p (b e) -> p b e", b=GROUP))\
                        .then_inc(gate_step, 1)
                    dve.wait_ge(gate_step, at + 1)
                    if needed(g):
                        dve.wait_ge(alpha_exp, g)
                    dve.tensor_reduce(best[:, :], score[:, :, :], AX.X, ALU.max).then_inc(alpha_in, 1)
                    dve.wait_ge(alpha_in, g + 1)
                    dve.tensor_tensor(key[:, :, :], score[:, :, :], bcast(best[:, :], 2, E), ALU.is_equal)\
                        .then_inc(gate_step, 1)
                    dve.wait_ge(gate_step, at + 2)
                    dve.tensor_tensor(key[:, :, :], key[:, :, :], bcast(rank, 1, GROUP), ALU.mult).then_inc(gate_step, 1)
                    dve.wait_ge(gate_step, at + 3)
                    dve.tensor_reduce(kbest[:, :], key[:, :, :], AX.X, ALU.max).then_inc(gate_step, 1)
                    dve.wait_ge(gate_step, at + 4)
                    dve.tensor_tensor(key[:, :, :], key[:, :, :], bcast(kbest[:, :], 2, E), ALU.is_equal)\
                        .then_inc(gate_step, 1)
                if e == 4:
                    dve.wait_ge(gate_step, at + 5)
                    dve.wait_ge(alpha_exp, g + 1)
                    dve.tensor_tensor(gate[:, slot], key[:, :, :], bcast(alpha[:, :], 2, E), ALU.mult)\
                        .then_inc(gate_ready, 1)
                if e == 6:
                    dve.wait_ge(b2_mm, g + 1)
                    dve.scalar_tensor_tensor(acc[:, slot], xc[:, slot], 2.0, by_batch(mp[1][:, :]), ALU.mult, ALU.add)\
                        .then_inc(acc_ready, 1)

            def add_expert(i, k, slot):
                dve.wait_ge(y_mm, i + 1)
                if needed(i):
                    dve.wait_ge(y_read, i)
                for b in range(GROUP):
                    op = dve.scalar_tensor_tensor(acc[:, slot, b, :], yp[k % 2][:, b * C:(b + 1) * C],
                                                  gate[:, slot, b, k:k + 1], acc[:, slot, b, :], ALU.mult, ALU.add)
                op.then_inc(y_read, 1)

            def finish_a(g, slot):
                dve.wait_ge(y_read, (g + 1) * E)
                row_stats(dve, lambda b: acc[:, slot, b, :], stats[:, 1], mv[:, 1], vec, vec_at(g, 1), mark)

            def finish_b(g, slot):
                dve.wait_ge(pool_step, pool_at(g, 1) + 2)
                dve.wait_ge(stored[slot], 16 + 8 * (g - slot))
                normalise(dve, lambda b: res[:, slot, b, :], lambda b: acc[:, slot, b, :], mv[:, 1], rstd[:, 1])\
                    .then_inc(res_ready, 1)

            def head(g, slot):
                for e in range(E):
                    head_part(g, slot, e)

            def step(g, slot, more):
                for e in range(E):
                    i = g * E + e
                    if needed(i - 1):
                        dve.wait_ge(y_mm, i - 1)
                    for j in range(NF):
                        if RELU[j] == "dve":
                            dve.wait_ge(hid_mm, i * NF + j + 1)
                            dve.tensor_scalar(hid[:, e % 2, j, :], hp[j][:, :], bias1[:, e * NF + j:e * NF + j + 1], 0.0,
                                              ALU.add, ALU.max).then_inc(hid_dve, 1)
                    if e:
                        if e == 1:
                            dve.wait_ge(acc_ready, g + 1)
                        add_expert(i - 1, e - 1, slot)
                    elif not (isinstance(g, int) and g == 0):
                        add_expert(i - 1, E - 1, 1 - slot)
                        finish_a(g - 1, 1 - slot)
                    if e == 1 and not (isinstance(g, int) and g == 0):
                        finish_b(g - 1, 1 - slot)
                    if more:
                        head_part(g + 1, 1 - slot, e)

            def tail(g, slot):
                add_expert(g * E + E - 1, E - 1, slot)
                finish_a(g, slot)
                finish_b(g, slot)

            run(head, step, tail)(dve)

        @block.gpsimd
        def _(pool):
            pool.memset(power[:, :], -0.5).then_inc(power_set, 1)
            pool.wait_ge(power_set, 1)

            def head_part(g, slot, e):
                if e == 0:
                    if needed(g - 1):
                        pool.wait_ge(acc_ready, g - 1)
                    pool.tensor_copy(xc[:, slot], X[:, bass.ds(g * GROUP, GROUP), :]).then_inc(xc_ready, 1)
                    pool.wait_ge(vec, vec_at(g, 0) + 2 * GROUP)
                    pool.sem_inc(mark, 1)
                    inv_std(pool, power[:, :], mv[:, 0], rstd[:, 0], pool_step, pool_at(g, 0))

            def finish(g):
                pool.wait_ge(vec, vec_at(g, 1) + 2 * GROUP)
                pool.sem_inc(mark, 1)
                inv_std(pool, power[:, :], mv[:, 1], rstd[:, 1], pool_step, pool_at(g, 1))

            def head(g, slot):
                head_part(g, slot, 0)

            def step(g, slot, more):
                if not (isinstance(g, int) and g == 0):
                    finish(g - 1)
                if more:
                    head_part(g + 1, 1 - slot, 0)

            run(head, step, lambda g, slot: finish(g))(pool)



PHASES = ("ssm", "self", "mlp1", "cross", "mlp2", "mix", "gla", "narrow", "experts")


def decoder_kernel(nc, dram, weights, NB, S, CTX, E, out, phases=PHASES):
    ctx = ExitStack()
    with ctx:
        X, XB, XC = (ctx.enter_context(nc.sbuf_tensor(n, [P, NB, C], F32)) for n in ("X", "XB", "XC"))
        env = {"X": X, "XB": XB, "XC": XC, "NG": NB // GROUP, "S": S, "CTX": CTX, "E": E}
        env["x"] = dram["x"].rearrange("b t c -> t b c")
        env["xT"] = dram["xT"]
        env["ctx"] = dram["ctx"].rearrange("b s c -> s b c")
        env["ctxT"] = dram["ctxT"]
        result = out.rearrange("b t c -> t b c")
        W = lambda k: (dram["w_" + k], weights[k])
        if "ssm" in phases:
            ssm_phase(nc, env, "ssm", *W("ssm"))
        if "self" in phases:
            attention_phase(nc, env, "self", *W("self"), "self")
        if "mlp1" in phases:
            mlp_phase(nc, env, "mlp1", *W("mlp1"), last=False)
        if "cross" in phases:
            attention_phase(nc, env, "cross", *W("cross"), "cross")
        if "mlp2" in phases:
            mlp_phase(nc, env, "mlp2", *W("mlp2"), last=True)
        if "mix" in phases:
            channel_mix_phase(nc, env, "mix", *W("mix"))
        if "gla" in phases:
            linear_attention_phase(nc, env, "gla", *W("gla"))
        if "narrow" in phases:
            attention_phase(nc, env, "narrow", *W("narrow"), "narrow")
        if "experts" in phases:
            experts_phase(nc, env, "experts", *W("experts"), result)


def columns(v):
    return np.ascontiguousarray(np.asarray(v).reshape(-1, P).T)


def rows(v, times=1):
    return np.tile(np.asarray(v), (P, times))


def tiles(m):
    k = m.shape[0] // P
    return np.ascontiguousarray(np.asarray(m).reshape(k, P, -1).transpose(1, 0, 2)).reshape(P, -1)


def lay_out_weights(i):
    f = {k: np.asarray(v) for k, v in i.items()}
    ident = np.eye(P, dtype=np.float32)
    at = np.arange(P)
    out = {}

    w = out["ssm"] = Weights()
    a = lambda k: f["L0_attn_" + k]
    w.add("ident", ident)
    w.add("w_in", a("W_in").T)
    w.add("b_in", columns(a("b_in")))
    R = a("W_dt").shape[1]
    order = np.concatenate([np.arange(R, R + 32)] * 3 + [np.arange(R)])
    w.add("w_x", tiles(a("W_x")[order].T))
    w.add("b_x", a("b_x")[order][:, None])
    w_dt = np.zeros((P, a("W_dt").shape[0]), np.float32)
    w_dt[96:96 + R] = a("W_dt").T
    w.add("w_dt", w_dt)
    w.add("b_dt", columns(a("b_dt")))
    w.add("a_log", tiles(a("A_log")))
    w.add("d_skip", columns(a("D")))
    w.add("w_out", tiles(a("W_out").T))
    w.add("bor", rows(a("b_out"), GROUP))
    w.add("pick", (at[:96, None] % 32 == np.arange(32)[None, :]).astype(np.float32))

    for kind, k in (("self", "a1_"), ("cross", "a2_")):
        w = out[kind] = Weights()
        a = lambda n: f["L0_xattn_" + k + n]
        flat = lambda m: m.transpose(1, 0, 2).reshape(m.shape[1], -1)
        w.add("ident", ident)
        w.add("wq", flat(a("wq")))
        w.add("wk", flat(a("wk")))
        w.add("wv", flat(a("wv")))
        w.add("wo", tiles(a("li1_w")))
        w.add("bor", rows(a("li1_b"), GROUP))
        w.add("gx", a("lnx_g")[:, None])
        w.add("bx", a("lnx_b")[:, None])
        w.add("gy", a("lny_g")[:, None])
        w.add("by", a("lny_b")[:, None])
        w.add("by128", np.repeat(a("lny_b")[:, None], P, axis=1))
        if kind == "self":
            w.add("g1r", rows(f["L0_xattn_ln1_g"], GROUP))
            w.add("be1r", rows(f["L0_xattn_ln1_b"], GROUP))
            w.add("mask", (at[:, None] > at[None, :]).astype(np.float32))
        m = out["mlp1" if kind == "self" else "mlp2"] = Weights()
        m.add("ident", ident)
        m.add("w2", a("li2_w"))
        m.add("b2", columns(a("li2_b")))
        m.add("w3", tiles(a("li3_w")))
        m.add("b3r", rows(a("li3_b"), GROUP))
        m.add("g3", a("ln3_g")[:, None])
        m.add("be3", a("ln3_b")[:, None])
        if kind == "self":
            m.add("g2r", rows(f["L0_xattn_ln2_g"], GROUP))
            m.add("be2r", rows(f["L0_xattn_ln2_b"], GROUP))

    w = out["mix"] = Weights()
    a = lambda k: f["L0_ffn_" + k]
    w.add("ident", ident)
    w.add("wr", a("W_r").T)
    w.add("wr_prev", a("W_r").T)
    w.add("wk", a("W_k").T)
    w.add("wk_prev", a("W_k").T)
    w.add("wv", a("W_v").T)
    w.add("mu_r", a("mu_r")[:, None])
    w.add("mu_k", a("mu_k")[:, None])

    w = out["gla"] = Weights()
    a = lambda k: f["L1_attn_" + k]
    heads = (at[:, None] // 8 == np.arange(16)[None, :]).astype(np.float32)
    gw, sw = np.zeros((P, 16), np.float32), np.zeros((P, 16), np.float32)
    for h in range(16):
        gw[8 * h:8 * h + 8, h] = a("gw_w")[0]
        sw[8 * h:8 * h + 8, h] = a("sw_w")[0]
    w.add("ident", ident)
    w.add("wq", a("q1_w").T)
    w.add("wk", a("k1_w").T)
    w.add("wk2", a("k2_w").T)
    w.add("gw", gw)
    w.add("sw", sw)
    w.add("wo", a("c_proj_w").T)
    w.add("tri", (at[:, None] <= at[None, :]).astype(np.float32))
    w.add("tri0", (at[:, None] < at[None, :]).astype(np.float32))
    w.add("up", (at[:, None] == at[None, :] + 1).astype(np.float32))
    w.add("heads", heads)

    w = out["narrow"] = Weights()
    a = lambda k: f["L1_xattn_" + k]
    w.add("ident", ident)
    w.add("wq", a("Wq"))
    w.add("wk", a("Wk"))
    w.add("wv", a("Wv"))
    w.add("wo", a("Wo"))
    w.add("bor", rows(a("bo"), GROUP))
    w.add("bq", a("bq")[:, None])
    w.add("bk", a("bk")[:, None])
    w.add("bvr", rows(a("bv")))
    w.add("heads", heads)

    w = out["experts"] = Weights()
    a = lambda k: f["L1_ffn_" + k]
    E, F, _ = a("W1").shape
    w.add("ident", ident)
    w.add("cen", a("centroids").T)
    w.add("gamma", a("gamma").T)
    w.add("beta", a("beta").T)
    w.add("w1", a("W1").transpose(2, 0, 1).reshape(C, E * F))
    w.add("b1", columns(a("b1").reshape(-1)))
    w.add("w2", tiles(a("W2").transpose(0, 2, 1).reshape(E * F, C)))
    w.add("b2", a("b2"))
    w.add("rank", rows(np.arange(E, 0, -1).astype(np.float32)))
    return out


def prepare(nc, i, phases=PHASES):
    x, c = np.asarray(i["x"]), np.asarray(i["ctx_512"])
    arrays = {
        "x": x,
        "xT": np.ascontiguousarray(x.transpose(2, 0, 1)).reshape(C, -1),
        "ctx": c,
        "ctxT": np.ascontiguousarray(c.transpose(2, 0, 1)).reshape(c.shape[2], -1),
    }
    weights = lay_out_weights(i)
    for k, w in weights.items():
        arrays["w_" + k] = w.packed()
        w.parts = None
    arrays = {f"in_{k}": np.ascontiguousarray(v) for k, v in arrays.items()}
    dram = {k[3:]: nc.dram_tensor(k, v.shape, F32, kind="ExternalInput").ap() for k, v in arrays.items()}
    out = nc.dram_tensor("out", x.shape, F32, kind="ExternalOutput").ap()
    decoder_kernel(nc, dram, weights, x.shape[0], c.shape[1], c.shape[2], np.asarray(i["L1_ffn_gamma"]).shape[0],
                   out, phases)
    return arrays


def kernel(**inputs):
    import concourse.bacc as _bacc
    from concourse.bass_utils import run_bass_kernel_spmd as _run

    nc = _bacc.Bacc("TRN2", target_bir_lowering=False, num_devices=1)
    arrays = prepare(nc, inputs)
    r = _run(nc, [arrays], core_ids=[0])
    return r.results[0]["out"]
```
